# Optimizing a Trainium2 kernel written in Bass

```python
import numpy as np
import jax
import jax.numpy as jnp

def _softmax(x, axis=-1):
    return jax.nn.softmax(x, axis=axis)

def _gelu(x):
    return jax.nn.gelu(x, approximate=True)

def _silu(x):
    return jax.nn.silu(x)

def _sigmoid(x):
    return jax.nn.sigmoid(x)

def _layernorm(x, axis=-1, eps=1e-05):
    m = jnp.mean(x, axis=axis, keepdims=True)
    v = jnp.var(x, axis=axis, keepdims=True)
    return (x - m) / jnp.sqrt(v + eps)

def _scatter_add(tgt, idx, src, axis=0):
    return tgt.at[idx].add(src)

def _segment_sum(src, seg, n):
    return jax.ops.segment_sum(src, seg, n)
kernel_name = 'mk_seq_preln_d1_jaxref_r4_cb5bee'

def setup_inputs(seed: int=0):
    np.random.seed(seed)
    _w = jnp.asarray

    def _L0_attn_setup():
        import jax, jax.numpy as jnp
        import numpy as np
        H = 256
        F = 1024
        B, S = (4, 1024)
        EPS = 1e-05

        def _layernorm(x, scale, bias):
            mu = jnp.mean(x, axis=-1, keepdims=True)
            var = jnp.var(x, axis=-1, keepdims=True)
            return (x - mu) * jax.lax.rsqrt(var + EPS) * scale + bias
        key = jax.random.key(seed)
        ks = jax.random.split(key, 4)
        x = jax.random.normal(ks[0], (B, S, H), dtype=jnp.float32)
        W_ret = jax.random.normal(ks[1], (H, H), dtype=jnp.float32) * 0.02
        b_ret = jnp.zeros((H,), dtype=jnp.float32)
        ln1_scale = jnp.ones((H,), dtype=jnp.float32)
        ln1_bias = jnp.zeros((H,), dtype=jnp.float32)
        W1 = jax.random.normal(ks[2], (H, F), dtype=jnp.float32) * 0.02
        b1 = jnp.zeros((F,), dtype=jnp.float32)
        W2 = jax.random.normal(ks[3], (F, H), dtype=jnp.float32) * 0.02
        b2 = jnp.zeros((H,), dtype=jnp.float32)
        ln2_scale = jnp.ones((H,), dtype=jnp.float32)
        ln2_bias = jnp.zeros((H,), dtype=jnp.float32)
        return {'x': x, 'W_ret': W_ret, 'b_ret': b_ret, 'ln1_scale': ln1_scale, 'ln1_bias': ln1_bias, 'W1': W1, 'b1': b1, 'W2': W2, 'b2': b2, 'ln2_scale': ln2_scale, 'ln2_bias': ln2_bias}
    _L0_attn_in = _L0_attn_setup()

    def _L0_ffn_setup():
        import jax, jax.numpy as jnp
        import numpy as np
        EPS = 1e-06
        LN_EPS = 1e-05

        def _absmean_core(W):
            gamma = jnp.mean(jnp.abs(W)) + EPS
            Ws = W / gamma
            Wq = jnp.sign(Ws) * jnp.minimum(jnp.round(jnp.abs(Ws)), 1.0)
            return (Wq, gamma)

        @jax.custom_vjp
        def absmean(W):
            return _absmean_core(W)[0]

        def _absmean_fwd(W):
            Wq, gamma = _absmean_core(W)
            return (Wq, gamma)

        def _absmean_bwd(gamma, g):
            return (g / gamma,)
        absmean.defvjp(_absmean_fwd, _absmean_bwd)

        def layernorm(x, w, b, eps=LN_EPS):
            mu = jnp.mean(x, axis=-1, keepdims=True)
            var = jnp.mean((x - mu) ** 2, axis=-1, keepdims=True)
            return (x - mu) * jax.lax.rsqrt(var + eps) * w + b
        key = jax.random.key(seed)
        k1, k2, k3 = jax.random.split(key, 3)
        d, h = (256, 1024)
        B, T = (8, 512)
        return {'x': jax.random.normal(k1, (B, T, d), jnp.float32), 'W_fc': jax.random.normal(k2, (h, d), jnp.float32), 'ln_w': jnp.ones((h,), jnp.float32), 'ln_b': jnp.zeros((h,), jnp.float32), 'W_proj': jax.random.normal(k3, (d, h), jnp.float32)}
    _L0_ffn_in = _L0_ffn_setup()
    _d = {'L0_attn_x': _L0_attn_in['x'], 'L0_attn_W_ret': _L0_attn_in['W_ret'], 'L0_attn_b_ret': _L0_attn_in['b_ret'], 'L0_attn_ln1_scale': _L0_attn_in['ln1_scale'], 'L0_attn_ln1_bias': _L0_attn_in['ln1_bias'], 'L0_attn_W1': _L0_attn_in['W1'], 'L0_attn_b1': _L0_attn_in['b1'], 'L0_attn_W2': _L0_attn_in['W2'], 'L0_attn_b2': _L0_attn_in['b2'], 'L0_attn_ln2_scale': _L0_attn_in['ln2_scale'], 'L0_attn_ln2_bias': _L0_attn_in['ln2_bias'], 'L0_ffn_W_fc': _L0_ffn_in['W_fc'], 'L0_ffn_ln_w': _L0_ffn_in['ln_w'], 'L0_ffn_ln_b': _L0_ffn_in['ln_b'], 'L0_ffn_W_proj': _L0_ffn_in['W_proj']}
    _x0 = _d['L0_attn_x']
    _d['L0_attn_x'] = jax.random.normal(jax.random.fold_in(jax.random.key(seed), 1), (16, 1024, 256), dtype=_x0.dtype)
    del _x0
    return _d

def reference(L0_attn_x, L0_attn_W_ret, L0_attn_b_ret, L0_attn_ln1_scale, L0_attn_ln1_bias, L0_attn_W1, L0_attn_b1, L0_attn_W2, L0_attn_b2, L0_attn_ln2_scale, L0_attn_ln2_bias, L0_ffn_W_fc, L0_ffn_ln_w, L0_ffn_ln_b, L0_ffn_W_proj):

    def _L0_attn_ref(x, W_ret, b_ret, ln1_scale, ln1_bias, W1, b1, W2, b2, ln2_scale, ln2_bias):
        import jax, jax.numpy as jnp
        import numpy as np
        H = 256
        F = 1024
        B, S = (4, 1024)
        EPS = 1e-05

        def _layernorm(x, scale, bias):
            mu = jnp.mean(x, axis=-1, keepdims=True)
            var = jnp.var(x, axis=-1, keepdims=True)
            return (x - mu) * jax.lax.rsqrt(var + EPS) * scale + bias
        sig = jax.nn.sigmoid(jnp.einsum('bsh,hk->bsk', x, W_ret) + b_ret)

        def ema_step(carry, s_t):
            xi = 0.5 * s_t + 0.5 * carry
            return (xi, xi)
        _, ret = jax.lax.scan(ema_step, jnp.zeros((x.shape[0], x.shape[2]), x.dtype), jnp.transpose(sig, (1, 0, 2)))
        retention_output = jnp.transpose(ret, (1, 0, 2))
        h = _layernorm(x + retention_output, ln1_scale, ln1_bias)
        ffn = jnp.einsum('bsf,fh->bsh', jax.nn.gelu(jnp.einsum('bsh,hf->bsf', h, W1) + b1), W2) + b2
        out = _layernorm(h + ffn, ln2_scale, ln2_bias)
        return out

    def _L0_ffn_ref(x, W_fc, ln_w, ln_b, W_proj):
        import jax, jax.numpy as jnp
        import numpy as np
        EPS = 1e-06
        LN_EPS = 1e-05

        def _absmean_core(W):
            gamma = jnp.mean(jnp.abs(W)) + EPS
            Ws = W / gamma
            Wq = jnp.sign(Ws) * jnp.minimum(jnp.round(jnp.abs(Ws)), 1.0)
            return (Wq, gamma)

        @jax.custom_vjp
        def absmean(W):
            return _absmean_core(W)[0]

        def _absmean_fwd(W):
            Wq, gamma = _absmean_core(W)
            return (Wq, gamma)

        def _absmean_bwd(gamma, g):
            return (g / gamma,)
        absmean.defvjp(_absmean_fwd, _absmean_bwd)

        def layernorm(x, w, b, eps=LN_EPS):
            mu = jnp.mean(x, axis=-1, keepdims=True)
            var = jnp.mean((x - mu) ** 2, axis=-1, keepdims=True)
            return (x - mu) * jax.lax.rsqrt(var + eps) * w + b
        h = jnp.einsum('btd,hd->bth', x, absmean(W_fc))
        h = jax.nn.gelu(h, approximate=False)
        h = layernorm(h, ln_w, ln_b)
        return jnp.einsum('bth,dh->btd', h, absmean(W_proj))
    x = L0_attn_x
    x = x + _L0_attn_ref(_layernorm(x, axis=-1), L0_attn_W_ret, L0_attn_b_ret, L0_attn_ln1_scale, L0_attn_ln1_bias, L0_attn_W1, L0_attn_b1, L0_attn_W2, L0_attn_b2, L0_attn_ln2_scale, L0_attn_ln2_bias)
    x = x + _L0_ffn_ref(_layernorm(x, axis=-1), L0_ffn_W_fc, L0_ffn_ln_w, L0_ffn_ln_b, L0_ffn_W_proj)
    return x

_drawn_inputs = setup_inputs


def setup_inputs(seed=0):
    import zlib

    import numpy as np

    out = dict(_drawn_inputs(seed))
    spreads = {'L0_attn_b_ret': (0.0, 0.589),
     'L0_attn_ln1_scale': (1.0, 0.2),
     'L0_attn_ln1_bias': (0.0, 0.1),
     'L0_attn_b1': (0.0, 0.368),
     'L0_attn_b2': (0.0, 0.1),
     'L0_attn_ln2_scale': (1.0, 0.2),
     'L0_attn_ln2_bias': (0.0, 0.1),
     'L0_ffn_ln_w': (1.0, 0.2),
     'L0_ffn_ln_b': (0.0, 0.1)}
    factors = {}
    for name, (base, spread) in spreads.items():
        noise = np.random.default_rng([zlib.crc32(name.encode()), seed]).standard_normal(out[name].shape)
        drawn = base * np.exp(spread * noise) if base else spread * noise
        out[name] = jnp.asarray(drawn.astype(out[name].dtype))
    for name, factor in factors.items():
        out[name] = (out[name] * factor).astype(out[name].dtype)
    return out
```

```python
from contextlib import ExitStack

import concourse.bass as bass
from concourse import mybir

F32 = mybir.dt.float32
F16 = mybir.dt.float16
U32 = mybir.dt.uint32
ALU = mybir.AluOpType
ACT = mybir.ActivationFunctionType
AX_X = mybir.AxisListType.X

P = 128
H = 256
F = 1024
KC = H // P
FC = F // P
TILES = 4
TOK = TILES * P
HALF = 512
NG = 4
LAG = 2
NORM_SCALE = 2.0 ** 10
PART_SCALE = 2.0 ** 14
GATE_SCALE = 2.0 ** 6
EPS = 1e-5


class Step:

    def __init__(self, pair, offset):
        self.pair, self.offset = pair, offset

    def shift(self, n):
        return Step(self.pair, self.offset + n)

    @property
    def parity(self):
        return self.offset % 2

    def value(self, per, n):
        return self.pair * (2 * per) + (self.offset * per + n)


def preln_retention_ffn_ternary_kernel(nc, x, W_ret, b_ret, ln1_scale, ln1_bias, W1, b1, W2, b2,
                                       ln2_scale, ln2_bias, W_fc, ln_w, ln_b, W_proj, out):
    B, S, _ = x.shape
    BLOCKS = B * S // TOK
    assert S == 2 * TOK and BLOCKS % 2 == 0
    x_flat = x.rearrange("b s d -> (b s) d")
    out_flat = out.rearrange("b s d -> (b s) d")

    with ExitStack() as ctx:
        def sb(name, shape, dt=F32):
            return ctx.enter_context(nc.sbuf_tensor(name, shape, dt))

        def sem(name):
            return ctx.enter_context(nc.semaphore(name))

        wret_hi, wret_lo = sb("wret_hi", [P, KC, H], F16), sb("wret_lo", [P, KC, H], F16)
        w1_hi, w1_lo = sb("w1_hi", [P, KC, F], F16), sb("w1_lo", [P, KC, F], F16)
        w2_hi, w2_lo = sb("w2_hi", [P, FC, H], F16), sb("w2_lo", [P, FC, H], F16)
        qfc = sb("qfc", [P, KC, F], F16)
        qproj = sb("qproj", [P, FC, H], F16)
        wret_raw, w1_raw = sb("wret_raw", [P, KC, H]), sb("w1_raw", [P, KC, F])
        wfc_raw, wproj_raw = sb("wfc_raw", [P, FC, H]), sb("wproj_raw", [P, KC, F])
        bret_col, s1_col, bias1_col = sb("bret_col", [P, KC]), sb("s1_col", [P, KC]), sb("bias1_col", [P, KC])
        b1_col, lnw_col, lnb_col = sb("b1_col", [P, FC]), sb("lnw_col", [P, FC]), sb("lnb_col", [P, FC])
        s1_row, hbias_row, b2_row = sb("s1_row", [P, H]), sb("hbias_row", [P, H]), sb("b2_row", [P, H])
        s2_row, bias2_row = sb("s2_row", [P, H]), sb("bias2_row", [P, H])
        cs_row, bp_row = sb("cs_row", [P, H]), sb("bp_row", [P, H])
        gate_col = sb("gate_col", [P, FC])
        ident, ones = sb("ident", [P, P]), sb("ones", [P, P])
        halves = sb("halves", [P, TOK])
        expo = sb("expo", [P, TILES])
        abs_sum = sb("abs_sum", [P, 2])
        thr, nthr = sb("thr", [P, 2]), sb("nthr", [P, 2])
        peak, peak_all = sb("peak", [P, 5]), sb("peak_all", [P, 5])
        pow2, ipow2 = sb("pow2", [P, 5]), sb("ipow2", [P, 5])
        part_inv = sb("part_inv", [P, 5])
        ret_scale, w1_scale, w2_scale, gate_back = (sb(n, [P, 1]) for n in
                                                    ("ret_scale", "w1_scale", "w2_scale", "gate_back"))
        x_in, x_bias = sb("x_in", [P, 2, TILES, H]), sb("x_bias", [P, 2, TILES, H])
        x0, hs, xhat = sb("x0", [P, TILES, H]), sb("hs", [P, TILES, H]), sb("xhat", [P, TILES, H])
        h_res = sb("h_res", [P, 2, TILES, H])
        z = sb("z", [P, TILES, H])
        zn = sb("zn", [P, TILES, H])
        x1, x2 = sb("x1", [P, 2, TILES, H]), sb("x2", [P, TILES, H])
        g2 = sb("g2", [P, TILES, F])
        D, y = sb("D", [P, TILES, H]), sb("y", [P, 2, TILES, H])
        x0T_hi, x0T_lo = sb("x0T_hi", [P, KC, TOK], F16), sb("x0T_lo", [P, KC, TOK], F16)
        xhT_hi, xhT_lo = sb("xhT_hi", [P, KC, TOK], F16), sb("xhT_lo", [P, KC, TOK], F16)
        x2T_hi, x2T_lo = sb("x2T_hi", [P, KC, TOK], F16), sb("x2T_lo", [P, KC, TOK], F16)
        tanh, ret = sb("tanh", [P, KC, TOK]), sb("ret", [P, 2, KC, TOK])
        g1T_hi, g1T_lo = sb("g1T_hi", [P, FC, TOK], F16), sb("g1T_lo", [P, FC, TOK], F16)
        g2T_hi, g2T_lo = sb("g2T_hi", [P, FC, TOK], F16), sb("g2T_lo", [P, FC, TOK], F16)
        def over(buffer, pattern, **sizes):
            return buffer[:].rearrange(pattern, **sizes)

        scratch = g2[:, 0:2].rearrange("p t n -> p (t n)")
        below = g2[:, 2:4].rearrange("p t n -> p (t n)")
        qproj_f = over(y, "p s t n -> p (s t) n")
        w2_raw = over(x1, "p s t n -> p (s t) n")
        lhs_bc = over(h_res, "p s t (e n) -> p (s t e) n", n=P)
        LN = ("x", "h", "z", "1", "g")
        bn = {n: sb(f"bn_{n}", [P, TILES, 12 if n == "g" else 6]) for n in LN}
        mv = {n: sb(f"mv_{n}", [P, TILES, 2]) for n in LN}
        neg_mean = {n: sb(f"neg_mean_{n}", [P, TILES]) for n in LN}
        var_eps = {n: sb(f"var_eps_{n}", [P, TILES]) for n in LN}
        rstd = {n: sb(f"rstd_{n}", [P, TILES]) for n in LN}
        g_back = sb("g_back", [P, 2, TILES])
        neg_mean_g = sb("neg_mean_g2", [P, 2, TILES])

        acc = [ctx.enter_context(nc.psum_tensor(f"acc{j}", [P, 2, H], F32)) for j in range(2)]
        ring = [ctx.enter_context(nc.psum_tensor(f"ring{j}", [P, HALF], F32)) for j in range(NG)]
        front = [ctx.enter_context(nc.psum_tensor(f"front{j}", [P, HALF], F32)) for j in range(2)]

        w_loaded, v_loaded = sem("w_loaded"), sem("v_loaded")
        pool_setup, dve_setup, act_setup, pe_setup = (sem(n) for n in
                                                      ("pool_setup", "dve_setup", "act_setup", "pe_setup"))
        x_loaded, y_stored = [sem("x_loaded0"), sem("x_loaded1")], [sem("y_stored0"), sem("y_stored1")]
        bn_done = {n: sem(f"bn_done_{n}") for n in LN}
        mv_done = {n: sem(f"mv_done_{n}") for n in LN}
        st_ready = {n: sem(f"st_ready_{n}") for n in LN}
        rs_done = {n: sem(f"rs_done_{n}") for n in LN}
        x0_ready, xbias_ready = sem("x0_ready"), sem("xbias_ready")
        x0_transposed, x0_hi, x0_lo = sem("x0_transposed"), sem("x0_hi"), sem("x0_lo")
        gates_ready, tanh_ready, scan_ready = sem("gates_ready"), sem("tanh_ready"), sem("scan_ready")
        ret_back, hs_ready = sem("ret_back"), sem("hs_ready")
        xhat_ready, hmul_done, hres_ready = sem("xhat_ready"), sem("hmul_done"), sem("hres_ready")
        xh_transposed, xh_hi, xh_lo = sem("xh_transposed"), sem("xh_hi"), sem("xh_lo")
        up1, gelu1, g1_hi, g1_lo = sem("up1"), sem("gelu1"), sem("g1_hi"), sem("g1_lo")
        down1, z_ready = sem("down1"), sem("z_ready")
        zn_done, zmul_done, x1_ready = sem("zn_done"), sem("zmul_done"), sem("x1_ready")
        x2_ready, x1b_ready, gback_ready = sem("x2_ready"), sem("x1b_ready"), sem("gback_ready")
        x2_transposed, x2_hi, x2_lo = sem("x2_transposed"), sem("x2_hi"), sem("x2_lo")
        up2, gelu2 = sem("up2"), sem("gelu2")
        g2_transposed, g2_hi, g2_lo = sem("g2_transposed"), sem("g2_hi"), sem("g2_lo")
        down2, centred, y_ready = sem("down2"), sem("centred"), sem("y_ready")

        block = ctx.enter_context(nc.Block())

        def steps(engine, step):
            step(Step(0, -1))
            step(Step(0, 0))
            with engine.Fori(0, BLOCKS // 2 - 1) as pair:
                step(Step(pair, 1), middle=True)
                step(Step(pair, 2), middle=True)
            step(Step(0, BLOCKS - 1))
            step(Step(0, BLOCKS))
            step(Step(0, BLOCKS + 1))

        def wait_alone(engine, past, past_value, semaphore, value):
            if not isinstance(value, int):
                engine.compute_val(value)
            engine.wait_ge(past, past_value)
            engine.wait_ge(semaphore, value)

        def runs(k, middle, shift):
            return middle or 0 <= k.offset + shift < BLOCKS

        @block.sync
        def _(sp):
            def load(k):
                sp.dma_start(x_in[:, k.parity], x_flat[bass.ts(k.value(1, 0), TOK), :]
                             .rearrange("(t p) d -> p t d", p=P)).then_inc(x_loaded[k.parity], 16)

            load(Step(0, 0))
            load(Step(0, 1))
            for dst, src in ((wfc_raw, W_fc.rearrange("(c p) d -> p c d", p=P)),
                             (wproj_raw, W_proj.rearrange("(c p) d -> p c d", p=P)),
                             (w1_raw, W1.rearrange("(c p) d -> p c d", p=P)),
                             (w2_raw, W2.rearrange("(c p) d -> p c d", p=P)),
                             (wret_raw, W_ret.rearrange("(c p) d -> p c d", p=P))):
                sp.dma_start(dst[:], src).then_inc(w_loaded, 16)

            def step(k, middle=False):
                if runs(k, middle, 2) and (middle or k.offset >= 0):
                    if middle and k.offset == 2:
                        pass
                    sp.wait_ge(xbias_ready, k.value(1, 1))
                    load(k.shift(2))
                if runs(k, middle, -2):
                    b = k.shift(-2)
                    sp.wait_ge(y_ready, b.value(1, 1))
                    sp.dma_start(out_flat[bass.ts(b.value(1, 0), TOK), :].rearrange("(t p) d -> p t d", p=P),
                                 y[:, b.parity]).then_inc(y_stored[b.parity], 16)

            step(Step(0, -1))
            step(Step(0, 0))
            step(Step(0, 1))
            with sp.Fori(0, BLOCKS // 2 - 2) as pair:
                step(Step(pair, 2), middle=True)
                step(Step(pair, 3), middle=True)
            step(Step(0, BLOCKS - 2))
            step(Step(0, BLOCKS - 1))
            step(Step(0, BLOCKS))
            step(Step(0, BLOCKS + 1))
            for s in y_stored:
                sp.wait_ge(s, 16 * BLOCKS // 2)

        @block.gpsimd
        def _(pool):
            pool.memset(ident[:], 0.0).then_inc(pool_setup, 1)
            pool.memset(ones[:], 1.0).then_inc(pool_setup, 1)
            pool.memset(halves[:], 0.5).then_inc(pool_setup, 1)
            pool.memset(expo[:], -0.5).then_inc(pool_setup, 1)
            pool.wait_ge(pool_setup, 4)
            pool.affine_select(out=ident[:], in_=ident[:], compare_op=ALU.not_equal, fill=1.0,
                               base=0, pattern=[[-1, P]], channel_multiplier=1).then_inc(pool_setup, 1)
            pool.wait_ge(dve_setup, PEAKS)
            pool.partition_all_reduce(peak_all[:], peak[:], P, bass.bass_isa.ReduceOp.max)\
                .then_inc(pool_setup, 1)

            def inverse_root(n, b):
                pool.wait_ge(st_ready[n], b.value(1, 1))
                pool.tensor_tensor(rstd[n][:], var_eps[n][:], expo[:], ALU.pow).then_inc(rs_done[n], 1)
                wait_alone(pool, pool_setup, 6, rs_done[n], b.value(1, 1))

            def normalise(dst, src, n, done):
                for t in range(TILES):
                    last = pool.tensor_scalar(dst[:, t], src[:, t], neg_mean[n][:, t:t + 1],
                                              rstd[n][:, t:t + 1], ALU.add, ALU.mult)
                last.then_inc(done, 1)

            def over_tiles(row):
                return row[:, None, :].to_broadcast([P, TILES, H])

            def step(k, middle=False):
                if runs(k, middle, 1):
                    b = k.shift(1)
                    inverse_root("x", b)
                    normalise(x0, x_in[:, b.parity], "x", x0_ready)
                    pool.tensor_tensor(x_bias[:, b.parity], x_in[:, b.parity], over_tiles(bias2_row), ALU.add)\
                        .then_inc(xbias_ready, 1)
                if runs(k, middle, 0):
                    inverse_root("z", k)
                    normalise(zn, z, "z", zn_done)
                    pool.wait_ge(zn_done, k.value(1, 1))
                    pool.tensor_tensor(zn[:], zn[:], over_tiles(s2_row), ALU.mult).then_inc(zmul_done, 1)
                    pool.wait_ge(zmul_done, k.value(1, 1))
                    pool.tensor_tensor(x1[:, k.parity], zn[:], x_bias[:, k.parity], ALU.add)\
                        .then_inc(x1_ready, 1)
                if runs(k, middle, 1):
                    b = k.shift(1)
                    inverse_root("h", b)
                    normalise(xhat, hs, "h", xhat_ready)
                if runs(k, middle, -1):
                    b = k.shift(-1)
                    inverse_root("g", b)
                    pool.tensor_scalar(g_back[:, b.parity], rstd["g"][:], gate_back[:, 0:1], None, ALU.mult)\
                        .then_inc(gback_ready, 1)
                if runs(k, middle, 0):
                    inverse_root("1", k)
                    normalise(x2, x1[:, k.parity], "1", x2_ready)
                if runs(k, middle, 1):
                    b = k.shift(1)
                    pool.wait_ge(xhat_ready, b.value(1, 1))
                    pool.tensor_tensor(h_res[:, b.parity], xhat[:], over_tiles(s1_row), ALU.mult)\
                        .then_inc(hmul_done, 1)
                    pool.wait_ge(hmul_done, b.value(1, 1))
                    pool.tensor_tensor(h_res[:, b.parity], h_res[:, b.parity], over_tiles(hbias_row), ALU.add)\
                        .then_inc(hres_ready, 1)
                if runs(k, middle, 0):
                    pool.wait_ge(x2_ready, k.value(1, 1))
                    pool.tensor_tensor(x1[:, k.parity], x1[:, k.parity], over_tiles(bp_row), ALU.add)\
                        .then_inc(x1b_ready, 1)

            steps(pool, step)

        @block.scalar
        def _(act):
            cols = ((bret_col, b_ret), (s1_col, ln1_scale), (bias1_col, ln1_bias), (b1_col, b1),
                    (lnw_col, ln_w), (lnb_col, ln_b))
            rows = ((s1_row, ln1_scale), (hbias_row, ln1_bias), (b2_row, b2), (s2_row, ln2_scale),
                    (bias2_row, ln2_bias))
            for dst, src in cols:
                with nc.allow_non_contiguous_dma("a few hundred elements, once"):
                    act.dma_start(dst[:], src.rearrange("(c p) -> p c", p=P)).then_inc(v_loaded, 16)
            for dst, src in rows:
                act.dma_start(dst[:], src.partition_broadcast(P)).then_inc(v_loaded, 16)
            act.wait_ge(w_loaded, 16 * 5)
            act.activation(scratch, wfc_raw[:].rearrange("p c d -> p (c d)"), ACT.Abs,
                           accum_out=abs_sum[:, 0:1]).then_inc(act_setup, 1)
            act.wait_ge(act_setup, 1)
            act.activation(scratch, wproj_raw[:].rearrange("p c d -> p (c d)"), ACT.Abs,
                           accum_out=abs_sum[:, 1:2]).then_inc(act_setup, 1)
            act.wait_ge(dve_setup, SETUP_END)

            def high_parts(b, dst, transposed, done):
                for m in range(KC):
                    act.wait_ge(transposed, b.value(KC, m + 1))
                    act.activation(dst[:, m], front[m][:], ACT.Copy).then_inc(done, 1)

            def gelu_and_high(k, c):
                g = ring[c % NG]
                act.wait_ge(up1, k.value(FC, c + 1))
                act.activation(g[:], g[:], ACT.Gelu_apprx_tanh, bias=b1_col[:, c:c + 1],
                               scale=w1_scale[:, 0:1]).then_inc(gelu1, 1)
                act.wait_ge(gelu1, k.value(FC, c + 1))
                act.activation(g1T_hi[:, c], g[:], ACT.Copy, scale=part_inv[:, 4:5]).then_inc(g1_hi, 1)

            def step(k, middle=False):
                for c in range(FC):
                    if runs(k, middle, 0):
                        gelu_and_high(k, c)
                    if c == X2T_AT and runs(k, middle, -1):
                        high_parts(k.shift(-1), x2T_hi, x2_transposed, x2_hi)
                    if c == X0T_AT + LAG - 1 and runs(k, middle, 1):
                        high_parts(k.shift(1), x0T_hi, x0_transposed, x0_hi)
                    if c == GATES_AT + LAG - 1 and runs(k, middle, 1):
                        for m in range(KC):
                            act.wait_ge(gates_ready, k.shift(1).value(KC, m + 1))
                            act.activation(tanh[:, m], front[m][:], ACT.Tanh, bias=bret_col[:, m:m + 1],
                                           scale=ret_scale[:, 0:1]).then_inc(tanh_ready, 1)
                if runs(k, middle, -1):
                    b = k.shift(-1)
                    for u in range(2 * TILES):
                        t, half = divmod(u, 2)
                        act.wait_ge(up2, b.value(2 * TILES, u + 1))
                        act.activation(g2[:, t, half * HALF:(half + 1) * HALF], ring[u % NG][:], ACT.Gelu,
                                       scale=1.0 / NORM_SCALE).then_inc(gelu2, 1)
                    for c in range(FC):
                        act.wait_ge(g2_transposed, b.value(FC, c + 1))
                        act.activation(g2T_hi[:, c], ring[c % NG][:], ACT.Copy, scale=gate_col[:, c:c + 1])\
                            .then_inc(g2_hi, 1)
                if runs(k, middle, 1):
                    high_parts(k.shift(1), xhT_hi, xh_transposed, xh_hi)

            steps(act, step)

        @block.vector
        def _(dve):
            count = [0]

            def link(instruction):
                count[0] += 1
                instruction.then_inc(dve_setup, 1)
                dve.wait_ge(dve_setup, count[0])

            dve.wait_ge(w_loaded, 16 * 5)
            dve.wait_ge(v_loaded, 16 * 11)
            for kc in range(KC):
                link(dve.tensor_scalar(below[:, kc * F:(kc + 1) * F], w1_raw[:, kc], s1_col[:, kc:kc + 1], None,
                                       ALU.mult))
            w1_scaled = below.rearrange("p (c n) -> p c n", c=KC)
            dve.wait_ge(pe_setup, PE_BIAS)
            link(dve.tensor_tensor(b1_col[:], front[0][:, 0:FC], b1_col[:], ALU.add))
            for n, src in enumerate((wret_raw[:].rearrange("p c n -> p (c n)"), below,
                                     w2_raw[:].rearrange("p c n -> p (c n)"), lnw_col[:], b1_col[:])):
                link(dve.tensor_reduce(out=peak[:, n:n + 1], in_=src, axis=AX_X, op=ALU.max,
                                       apply_absolute_value=True))
            assert count[0] == PEAKS
            dve.wait_ge(pool_setup, 6)
            link(dve.scalar_tensor_tensor(peak_all[:, 4:5], peak_all[:, 1:2], float(H), peak_all[:, 4:5],
                                          ALU.mult, ALU.add))
            link(dve.tensor_scalar(peak_all[:], peak_all[:], 2.0 ** -60, None, ALU.max))
            link(dve.tensor_single_scalar(pow2[:].bitcast(U32), peak_all[:].bitcast(U32), 0x7F800000,
                                          ALU.bitwise_and))
            link(dve.reciprocal(ipow2[:], pow2[:]))
            link(dve.tensor_scalar(part_inv[:], ipow2[:], PART_SCALE, None, ALU.mult))
            link(dve.tensor_scalar(ret_scale[:], pow2[:, 0:1], 0.5 / (NORM_SCALE * PART_SCALE), None, ALU.mult))
            link(dve.tensor_scalar(w1_scale[:], pow2[:, 1:2], 1.0 / (NORM_SCALE * PART_SCALE), None, ALU.mult))
            link(dve.tensor_scalar(w2_scale[:], pow2[:, 2:3], pow2[:, 4:5], None, ALU.mult))
            link(dve.tensor_scalar(w2_scale[:], w2_scale[:], PART_SCALE ** -2, None, ALU.mult))
            link(dve.tensor_scalar(gate_back[:], pow2[:, 3:4], 1.0 / GATE_SCALE, None, ALU.mult))
            link(dve.tensor_scalar(gate_col[:], lnw_col[:], ipow2[:, 3:4], GATE_SCALE, ALU.mult, ALU.mult))
            link(dve.tensor_scalar(bret_col[:], bret_col[:], 0.5, None, ALU.mult))
            link(dve.tensor_scalar(s1_row[:], s1_row[:], 1.0 / NORM_SCALE, None, ALU.mult))
            link(dve.tensor_tensor(hbias_row[:], hbias_row[:], b2_row[:], ALU.add))
            for src, dst_hi, dst_lo, n in ((wret_raw, wret_hi, wret_lo, 0), (w1_scaled, w1_hi, w1_lo, 1),
                                           (w2_raw, w2_hi, w2_lo, 2)):
                link(dve.tensor_scalar(src[:], src[:], part_inv[:, n:n + 1], None, ALU.mult))
                link(dve.tensor_copy(dst_hi[:], src[:]))
                link(dve.tensor_tensor(dst_lo[:], src[:], dst_hi[:], ALU.subtract))
            dve.wait_ge(pe_setup, PE_SUMS)
            link(dve.tensor_scalar(thr[:], front[1][:, 0:2], 0.5 / (H * F), 0.5e-6, ALU.mult, ALU.add))
            link(dve.tensor_scalar(nthr[:], thr[:], -1.0, None, ALU.mult))
            for n, raw in enumerate((wfc_raw, wproj_raw)):
                flat = raw[:].rearrange("p c d -> p (c d)")
                link(dve.tensor_scalar(below, flat, nthr[:, n:n + 1], None, ALU.is_lt))
                link(dve.scalar_tensor_tensor(flat, flat, thr[:, n:n + 1], below, ALU.is_gt, ALU.subtract))
            assert count[0] == TERNARY
            for n in range(4):
                dve.wait_ge(pe_setup, PE_SUMS + n + 1)
                kc, c0 = n // 2, 4 * (n % 2)
                link(dve.tensor_copy(qfc[:, kc, c0 * P:(c0 + 4) * P], ring[n][:]))
            for n in range(4):
                dve.wait_ge(pe_setup, PE_SUMS + 4 + n + 1)
                link(dve.tensor_copy(qproj[:, 2 * n:2 * n + 2].rearrange("p c d -> p (c d)"), ring[n][:]))
                link(dve.tensor_copy(qproj_f[:, 2 * n:2 * n + 2].rearrange("p c d -> p (c d)"), ring[n][:]))
            for c in range(FC):
                link(dve.tensor_scalar(lhs_bc[:, c], ones[:], gate_col[:, c:c + 1], None, ALU.mult))
                link(dve.tensor_scalar(lhs_bc[:, FC + c], ones[:], lnb_col[:, c:c + 1], None, ALU.mult))
            assert count[0] == ROWS
            dve.wait_ge(pe_setup, PE_ROWS)
            link(dve.tensor_copy(cs_row[:], acc[0][:, 0]))
            link(dve.tensor_copy(bp_row[:], acc[1][:, 0]))
            assert count[0] == SETUP_END

            def statistics(n, b, src, var_scale, eps):
                for t in range(TILES):
                    last = dve.bn_stats(bn[n][:, t], src[:, t])
                last.then_inc(bn_done[n], 1)
                aggregate(n, b, var_scale, eps, neg_mean[n][:])

            def aggregate(n, b, var_scale, eps, neg):
                wait_alone(dve, dve_setup, SETUP_END, bn_done[n], b.value(1, 1))
                for t in range(TILES):
                    last = dve.bn_aggr(mv[n][:, t], bn[n][:, t])
                last.then_inc(mv_done[n], 1)
                dve.wait_ge(mv_done[n], b.value(1, 1))
                dve.tensor_scalar(neg, mv[n][:, :, 0], -1.0, None, ALU.mult)
                dve.tensor_scalar(var_eps[n][:], mv[n][:, :, 1], var_scale, eps, ALU.mult, ALU.add)\
                    .then_inc(st_ready[n], 1)

            def low_parts(b, dst_hi, dst_lo, hi_done, lo_done):
                for m in range(KC):
                    dve.wait_ge(hi_done, b.value(KC, m + 1))
                    dve.tensor_tensor(dst_lo[:, m], front[m][:], dst_hi[:, m], ALU.subtract).then_inc(lo_done, 1)

            def finish(b):
                dve.wait_ge(down2, b.value(1, 1))
                for t in range(TILES):
                    last = dve.scalar_tensor_tensor(D[:, t], cs_row[:], neg_mean_g[:, b.parity, t:t + 1],
                                                    acc[t // 2][:, t % 2], ALU.mult, ALU.add)
                last.then_inc(centred, 1)
                dve.wait_ge(centred, b.value(1, 1))
                dve.wait_ge(gback_ready, b.value(1, 1))
                dve.wait_ge(x1b_ready, b.value(1, 1))

            def finish_out(b):
                for t in range(TILES):
                    last = dve.scalar_tensor_tensor(y[:, b.parity, t], D[:, t], g_back[:, b.parity, t:t + 1],
                                                    x1[:, b.parity, t], ALU.mult, ALU.add)
                last.then_inc(y_ready, 1)

            def step(k, middle=False):
                if runs(k, middle, -2):
                    b = k.shift(-2)
                    finish(b)
                    if middle and k.offset < 4 or not middle and b.offset < 2:
                        pass
                    if not (not middle and b.offset < 2):
                        dve.wait_ge(y_stored[b.parity], stored_before(b))
                    finish_out(b)
                if runs(k, middle, 1):
                    b = k.shift(1)
                    dve.wait_ge(x_loaded[b.parity], loaded(b))
                    statistics("x", b, x_in[:, b.parity], NORM_SCALE ** -2, EPS * NORM_SCALE ** -2)
                for c in range(FC):
                    if runs(k, middle, 0):
                        dve.wait_ge(g1_hi, k.value(FC, c + 1))
                        dve.scalar_tensor_tensor(g1T_lo[:, c], ring[c % NG][:], part_inv[:, 4:5], g1T_hi[:, c],
                                                 ALU.mult, ALU.subtract).then_inc(g1_lo, 1)
                    if c == X2T_AT and runs(k, middle, -1):
                        low_parts(k.shift(-1), x2T_hi, x2T_lo, x2_hi, x2_lo)
                    if c == X0T_AT + LAG - 1 and runs(k, middle, 1):
                        low_parts(k.shift(1), x0T_hi, x0T_lo, x0_hi, x0_lo)
                    if c == FC - 2 and runs(k, middle, 1):
                        b = k.shift(1)
                        for m in range(KC):
                            dve.wait_ge(tanh_ready, b.value(KC, m + 1))
                            first = b.parity == 0
                            dve.tensor_tensor_scan(ret[:, b.parity, m], halves[:], tanh[:, m],
                                                   -2.0 if first else ret[:, 0, m, TOK - 1:TOK],
                                                   ALU.mult, ALU.add).then_inc(scan_ready, 1)
                if runs(k, middle, 0):
                    dve.wait_ge(down1, k.value(1, 1))
                    dve.wait_ge(hres_ready, k.value(1, 1))
                    for j in range(2):
                        dve.scalar_tensor_tensor(z[:, 2 * j:2 * j + 2], acc[j][:], w2_scale[:, 0:1],
                                                 h_res[:, k.parity, 2 * j:2 * j + 2], ALU.mult, ALU.add)\
                            .then_inc(z_ready, 1)
                    dve.wait_ge(z_ready, k.value(2, 2))
                    statistics("z", k, z, 1.0, EPS)
                for u in range(2 * TILES):
                    if runs(k, middle, -1):
                        t, half = divmod(u, 2)
                        dve.wait_ge(gelu2, k.shift(-1).value(2 * TILES, u + 1))
                        last = dve.bn_stats(bn["g"][:, t, 6 * half:6 * half + 6],
                                            g2[:, t, half * HALF:(half + 1) * HALF])
                    if u == RET_AT and runs(k, middle, 1):
                        b = k.shift(1)
                        for j in range(2):
                            dve.wait_ge(ret_back, b.value(2, j + 1))
                            dve.scalar_tensor_tensor(hs[:, 2 * j:2 * j + 2].rearrange("p t d -> p (t d)"),
                                                     front[j][:], NORM_SCALE / 4,
                                                     x0[:, 2 * j:2 * j + 2].rearrange("p t d -> p (t d)"),
                                                     ALU.mult, ALU.add).then_inc(hs_ready, 1)
                        dve.wait_ge(hs_ready, b.value(2, 2))
                        statistics("h", b, hs, NORM_SCALE ** -2, EPS)
                if runs(k, middle, -1):
                    last.then_inc(bn_done["g"], 1)
                    b = k.shift(-1)
                    aggregate("g", b, 1.0, EPS, neg_mean_g[:, b.parity])
                for c in range(FC):
                    if runs(k, middle, -1):
                        dve.wait_ge(g2_hi, k.shift(-1).value(FC, c + 1))
                        dve.scalar_tensor_tensor(g2T_lo[:, c], ring[c % NG][:], gate_col[:, c:c + 1],
                                                 g2T_hi[:, c], ALU.mult, ALU.subtract).then_inc(g2_lo, 1)
                    if c == STAT1_AT and runs(k, middle, 0):
                        dve.wait_ge(x1_ready, k.value(1, 1))
                        statistics("1", k, x1[:, k.parity], NORM_SCALE ** -2, EPS * NORM_SCALE ** -2)
                if runs(k, middle, 1):
                    low_parts(k.shift(1), xhT_hi, xhT_lo, xh_hi, xh_lo)

            def loaded(b):
                return b.pair * 16 + 16 * (b.offset // 2 + 1)

            def stored_before(b):
                return b.pair * 16 + 16 * (b.offset // 2)

            step(Step(0, -1))
            step(Step(0, 0))
            step(Step(0, 1))
            step(Step(0, 2))
            step(Step(0, 3))
            with dve.Fori(0, (BLOCKS - 4) // 2 - 1) as pair:
                step(Step(pair, 4), middle=True)
                step(Step(pair, 5), middle=True)
            step(Step(0, BLOCKS - 2))
            step(Step(0, BLOCKS - 1))
            step(Step(0, BLOCKS))
            step(Step(0, BLOCKS + 1))

        @block.tensor
        def _(pe):
            def transposes(src, rows, b_done):
                for m in range(KC):
                    for t in range(TILES):
                        last = pe.transpose(front[m][:, t * P:(t + 1) * P], src[:, t, m * P:(m + 1) * P], ident[:])
                    last.then_inc(b_done, 1)

            pe.wait_ge(w_loaded, 16 * 5)
            pe.wait_ge(v_loaded, 16 * 11)
            pe.wait_ge(pool_setup, 5)
            for c in range(FC):
                for kc in range(KC):
                    last = pe.matmul(front[0][:, c:c + 1], w1_raw[:, kc, c * P:(c + 1) * P], bias1_col[:, kc:kc + 1],
                                     start=(kc == 0), stop=(kc == KC - 1))
            last.then_inc(pe_setup, 1)
            pe.wait_ge(act_setup, 2)
            pe.matmul(front[1][:, 0:2], ones[:], abs_sum[:], start=True, stop=True).then_inc(pe_setup, 1)
            pe.wait_ge(dve_setup, TERNARY)
            for kc in range(KC):
                for c0 in (0, 4):
                    for c in range(c0, c0 + 4):
                        last = pe.transpose(ring[2 * kc + c0 // 4][:, (c - c0) * P:(c - c0 + 1) * P],
                                            wfc_raw[:, c, kc * P:(kc + 1) * P], ident[:])
                    last.then_inc(pe_setup, 1)
            for n in range(4):
                pe.wait_ge(dve_setup, TERNARY + n + 1)
                for c in (2 * n, 2 * n + 1):
                    for kc in range(KC):
                        last = pe.transpose(ring[n][:, ((c % 2) * KC + kc) * P:((c % 2) * KC + kc + 1) * P],
                                            wproj_raw[:, kc, c * P:(c + 1) * P], ident[:])
                last.then_inc(pe_setup, 1)
            pe.wait_ge(dve_setup, ROWS)
            for n in range(2):
                for c in range(FC):
                    last = pe.matmul(acc[n][:, 0], lhs_bc[:, n * FC + c], qproj_f[:, c],
                                     start=(c == 0), stop=(c == FC - 1))
            last.then_inc(pe_setup, 1)
            pe.wait_ge(dve_setup, SETUP_END)

            def three_passes(dst, parts, first=True, last=True, **kw):
                for n, (lhsT, rhs) in enumerate(parts):
                    mm = pe.matmul(dst, lhsT, rhs, start=first and n == 0, stop=last and n == len(parts) - 1, **kw)
                return mm

            def up_first(k, c):
                cols = slice(c * P, (c + 1) * P)
                three_passes(ring[c % NG][:], [
                    p for kc in range(KC) for p in ((w1_hi[:, kc, cols], xhT_hi[:, kc]),
                                                    (w1_hi[:, kc, cols], xhT_lo[:, kc]),
                                                    (w1_lo[:, kc, cols], xhT_hi[:, kc]))]).then_inc(up1, 1)

            def down_first(k, c):
                pe.wait_ge(g1_lo, k.value(FC, c + 1))
                for t in range(TILES):
                    cols = slice(t * P, (t + 1) * P)
                    mm = three_passes(acc[t // 2][:, t % 2], ((g1T_hi[:, c, cols], w2_hi[:, c]),
                                                              (g1T_hi[:, c, cols], w2_lo[:, c]),
                                                              (g1T_lo[:, c, cols], w2_hi[:, c])),
                                      first=c == 0 and t % 2 == 0, last=c == FC - 1, skip_group_check=True)
                if c == FC - 1:
                    mm.then_inc(down1, 1)

            def up_second(b, u):
                t, half = divmod(u, 2)
                if u >= NG:
                    pe.wait_ge(gelu2, b.value(2 * TILES, u - NG + 1))
                cols = slice(t * P, (t + 1) * P)
                three_passes(ring[u % NG][:], [
                    (part[:, kc, cols], qfc[:, kc, half * HALF:(half + 1) * HALF])
                    for kc in range(KC) for part in (x2T_hi, x2T_lo)]).then_inc(up2, 1)

            def transpose_second(b, c):
                for t in range(TILES):
                    last = pe.transpose(ring[c % NG][:, t * P:(t + 1) * P], g2[:, t, c * P:(c + 1) * P], ident[:])
                last.then_inc(g2_transposed, 1)

            def down_second(b, c):
                pe.wait_ge(g2_lo, b.value(FC, c + 1))
                for t in range(TILES):
                    cols = slice(t * P, (t + 1) * P)
                    mm = three_passes(acc[t // 2][:, t % 2], ((g2T_hi[:, c, cols], qproj[:, c]),
                                                              (g2T_lo[:, c, cols], qproj[:, c])),
                                      first=c == 0 and t % 2 == 0, last=c == FC - 1, skip_group_check=True)
                if c == FC - 1:
                    mm.then_inc(down2, 1)

            def step(k, middle=False):
                if runs(k, middle, 0):
                    pe.wait_ge(xh_lo, k.value(KC, KC))
                for c in range(FC + LAG):
                    if c < FC and runs(k, middle, 0):
                        up_first(k, c)
                    if c == X2T_AT and runs(k, middle, -1):
                        pe.wait_ge(x2_ready, k.shift(-1).value(1, 1))
                        if runs(k, middle, 0) or True:
                            pass
                        transposes(x2, None, x2_transposed)
                    if c >= LAG and runs(k, middle, 0):
                        if c == LAG and (middle or k.offset >= 2):
                            pe.wait_ge(centred, k.shift(-2).value(1, 1))
                        down_first(k, c - LAG)
                    if c == X0T_AT + LAG - 1 and runs(k, middle, 1):
                        if runs(k, middle, -1):
                            pe.wait_ge(x2_lo, k.shift(-1).value(KC, KC))
                        pe.wait_ge(x0_ready, k.shift(1).value(1, 1))
                        transposes(x0, None, x0_transposed)
                    if c == GATES_AT + LAG - 1 and runs(k, middle, 1):
                        pe.wait_ge(x0_lo, k.shift(1).value(KC, KC))
                        for m in range(KC):
                            cols = slice(m * P, (m + 1) * P)
                            three_passes(front[m][:], [
                                p for kc in range(KC) for p in ((wret_hi[:, kc, cols], x0T_hi[:, kc]),
                                                                (wret_hi[:, kc, cols], x0T_lo[:, kc]),
                                                                (wret_lo[:, kc, cols], x0T_hi[:, kc]))])\
                                .then_inc(gates_ready, 1)
                if runs(k, middle, -1):
                    pe.wait_ge(x2_lo, k.shift(-1).value(KC, KC))
                for u in range(2 * TILES):
                    if runs(k, middle, -1):
                        up_second(k.shift(-1), u)
                    if u == RET_AT and runs(k, middle, 1):
                        b = k.shift(1)
                        pe.wait_ge(scan_ready, b.value(KC, KC))
                        for t in range(TILES):
                            for m in range(KC):
                                mm = pe.transpose(front[t // 2][:, (t % 2) * H + m * P:(t % 2) * H + (m + 1) * P],
                                                  ret[:, b.parity, m, t * P:(t + 1) * P], ident[:])
                            if t % 2:
                                mm.then_inc(ret_back, 1)
                if runs(k, middle, -1):
                    pe.wait_ge(gelu2, k.shift(-1).value(2 * TILES, 2 * TILES))
                for c in range(FC + LAG):
                    if c < FC and runs(k, middle, -1):
                        transpose_second(k.shift(-1), c)
                    if c >= LAG and runs(k, middle, -1):
                        if c == LAG and runs(k, middle, 0):
                            pe.wait_ge(z_ready, k.value(2, 2))
                        down_second(k.shift(-1), c - LAG)
                    if c == XHAT_AT + LAG and runs(k, middle, 1):
                        pe.wait_ge(xhat_ready, k.shift(1).value(1, 1))
                        transposes(xhat, None, xh_transposed)

            steps(pe, step)


X2T_AT, X0T_AT, GATES_AT, RET_AT, XHAT_AT, STAT1_AT = 2, 3, 5, 3, 5, 4
PEAKS = KC + 1 + 5
TERNARY = PEAKS + 14 + 9 + 2 + 4
ROWS = TERNARY + 4 + 8 + 2 * FC
SETUP_END = ROWS + 2
PE_BIAS = 1
PE_SUMS = 2
PE_ROWS = PE_SUMS + 8 + 1


_INS = ["L0_attn_x", "L0_attn_W_ret", "L0_attn_b_ret", "L0_attn_ln1_scale", "L0_attn_ln1_bias", "L0_attn_W1",
        "L0_attn_b1", "L0_attn_W2", "L0_attn_b2", "L0_attn_ln2_scale", "L0_attn_ln2_bias", "L0_ffn_W_fc",
        "L0_ffn_ln_w", "L0_ffn_ln_b", "L0_ffn_W_proj"]
_OUTS = [((16, 1024, 256), "float32")]


def kernel(**inputs):
    import numpy as _np
    import concourse.bacc as _bacc
    from concourse import mybir as _mybir
    from concourse.bass_utils import run_bass_kernel_spmd as _run

    nc = _bacc.Bacc("TRN2", target_bir_lowering=False, num_devices=1)
    arrays, args = {}, []
    for name in _INS:
        a = _np.ascontiguousarray(inputs[name])
        arrays[f"in_{name}_dram"] = a
        args.append(nc.dram_tensor(f"in_{name}_dram", a.shape, _mybir.dt.from_np(a.dtype), kind="ExternalInput").ap())
    for i, (shape, dtype) in enumerate(_OUTS):
        dt = _mybir.dt.from_np(_np.dtype(dtype))
        args.append(nc.dram_tensor(f"out_{i}_dram", shape, dt, kind="ExternalOutput").ap())
    preln_retention_ffn_ternary_kernel(nc, *args)
    r = _run(nc, [arrays], core_ids=[0])
    got = tuple(r.results[0][f"out_{i}_dram"] for i in range(len(_OUTS)))
    return got[0]
```

```python
from contextlib import ExitStack

import concourse.bass as bass
from concourse import mybir

F32 = mybir.dt.float32
F16 = mybir.dt.float16
U32 = mybir.dt.uint32
ALU = mybir.AluOpType
ACT = mybir.ActivationFunctionType
AX_X = mybir.AxisListType.X

P = 128
H = 256
F = 1024
KC = H // P
FC = F // P
TILES = 4
TOK = TILES * P
HALF = 512
NG = 4
LAG = 2
LAG2 = 3
NORM_SCALE = 2.0 ** 10
PART_SCALE = 2.0 ** 14
GATE_SCALE = 2.0 ** 6
EPS = 1e-5


class Step:

    def __init__(self, pair, offset):
        self.pair, self.offset = pair, offset

    def shift(self, n):
        return Step(self.pair, self.offset + n)

    @property
    def parity(self):
        return self.offset % 2

    def value(self, per, n):
        return self.pair * (2 * per) + (self.offset * per + n)


def preln_retention_ffn_ternary_kernel(nc, x, W_ret, b_ret, ln1_scale, ln1_bias, W1, b1, W2, b2,
                                       ln2_scale, ln2_bias, W_fc, ln_w, ln_b, W_proj, out):
    B, S, _ = x.shape
    BLOCKS = B * S // TOK
    assert S == 2 * TOK and BLOCKS % 2 == 0
    x_flat = x.rearrange("b s d -> (b s) d")
    out_flat = out.rearrange("b s d -> (b s) d")

    with ExitStack() as ctx:
        def sb(name, shape, dt=F32):
            return ctx.enter_context(nc.sbuf_tensor(name, shape, dt))

        def sem(name):
            return ctx.enter_context(nc.semaphore(name))

        wret_hi, wret_lo = sb("wret_hi", [P, KC, H], F16), sb("wret_lo", [P, KC, H], F16)
        w1_hi, w1_lo = sb("w1_hi", [P, KC, F], F16), sb("w1_lo", [P, KC, F], F16)
        w2_hi, w2_lo = sb("w2_hi", [P, FC, H], F16), sb("w2_lo", [P, FC, H], F16)
        qfc = sb("qfc", [P, KC, F], F16)
        qproj = sb("qproj", [P, FC, H], F16)
        wret_raw, w1_raw = sb("wret_raw", [P, KC, H]), sb("w1_raw", [P, KC, F])
        wfc_raw, wproj_raw = sb("wfc_raw", [P, FC, H]), sb("wproj_raw", [P, KC, F])
        bret_col, s1_col, bias1_col = sb("bret_col", [P, KC]), sb("s1_col", [P, KC]), sb("bias1_col", [P, KC])
        b1_col, lnw_col, lnb_col = sb("b1_col", [P, FC]), sb("lnw_col", [P, FC]), sb("lnb_col", [P, FC])
        s1_row, hbias_row, b2_row = sb("s1_row", [P, H]), sb("hbias_row", [P, H]), sb("b2_row", [P, H])
        s2_row, bias2_row = sb("s2_row", [P, H]), sb("bias2_row", [P, H])
        cs_row, bp_row = sb("cs_row", [P, H]), sb("bp_row", [P, H])
        gate_col = sb("gate_col", [P, FC])
        ident, ones = sb("ident", [P, P]), sb("ones", [P, P])
        halves = sb("halves", [P, TOK])
        expo = sb("expo", [P, TILES])
        abs_sum = sb("abs_sum", [P, 2])
        thr, nthr = sb("thr", [P, 2]), sb("nthr", [P, 2])
        peak, peak_all = sb("peak", [P, 5]), sb("peak_all", [P, 5])
        pow2, ipow2 = sb("pow2", [P, 5]), sb("ipow2", [P, 5])
        part_inv = sb("part_inv", [P, 5])
        w1_peak, w1_inv = sb("w1_peak", [P, KC]), sb("w1_inv", [P, KC])
        ret_scale, w1_scale, w2_scale, gate_back = (sb(n, [P, 1]) for n in
                                                    ("ret_scale", "w1_scale", "w2_scale", "gate_back"))
        x_in, x_bias = sb("x_in", [P, 2, TILES, H]), sb("x_bias", [P, 2, TILES, H])
        x0, hs, xhat = sb("x0", [P, TILES, H]), sb("hs", [P, TILES, H]), sb("xhat", [P, TILES, H])
        h_res = sb("h_res", [P, 2, TILES, H])
        z = sb("z", [P, TILES, H])
        zn = sb("zn", [P, TILES, H])
        x1, x2 = sb("x1", [P, 2, TILES, H]), sb("x2", [P, TILES, H])
        g2 = sb("g2", [P, TILES, F])
        D, y = sb("D", [P, TILES, H]), sb("y", [P, 2, TILES, H])
        x0T_hi, x0T_lo = sb("x0T_hi", [P, KC, TOK], F16), sb("x0T_lo", [P, KC, TOK], F16)
        xhT_hi, xhT_lo = sb("xhT_hi", [P, KC, TOK], F16), sb("xhT_lo", [P, KC, TOK], F16)
        x2T_hi, x2T_lo = sb("x2T_hi", [P, KC, TOK], F16), sb("x2T_lo", [P, KC, TOK], F16)
        tanh, ret = sb("tanh", [P, KC, TOK]), sb("ret", [P, 2, KC, TOK])
        g1T_hi, g1T_lo = sb("g1T_hi", [P, FC, TOK], F16), sb("g1T_lo", [P, FC, TOK], F16)
        g2T_hi, g2T_lo = sb("g2T_hi", [P, FC, TOK], F16), sb("g2T_lo", [P, FC, TOK], F16)
        def over(buffer, pattern, **sizes):
            return buffer[:].rearrange(pattern, **sizes)

        scratch = [g2[:, 2 * n:2 * n + 2].rearrange("p t n -> p (t n)") for n in range(2)]
        qproj_f = over(y, "p s t n -> p (s t) n")
        w2_raw = over(x1, "p s t n -> p (s t) n")
        lhs_bc = [buffer[:].bitcast(F32).rearrange("p c (e n) -> p (c e) n", n=P)[:, 0:FC] for buffer in (g2T_hi, g2T_lo)]
        LN = ("x", "h", "z", "1", "g")
        bn = {n: sb(f"bn_{n}", [P, TILES, 12 if n == "g" else 6]) for n in LN}
        mv = {n: sb(f"mv_{n}", [P, TILES, 2]) for n in LN}
        neg_mean = {n: sb(f"neg_mean_{n}", [P, TILES]) for n in LN}
        var_eps = {n: sb(f"var_eps_{n}", [P, TILES]) for n in LN}
        rstd = {n: sb(f"rstd_{n}", [P, TILES]) for n in LN}
        g_back = sb("g_back", [P, 2, TILES])
        neg_mean_g = sb("neg_mean_g2", [P, 2, TILES])

        acc = [ctx.enter_context(nc.psum_tensor(f"acc{j}", [P, 2, H], F32)) for j in range(2)]
        ring = [ctx.enter_context(nc.psum_tensor(f"ring{j}", [P, HALF], F32)) for j in range(NG)]
        front = [ctx.enter_context(nc.psum_tensor(f"front{j}", [P, HALF], F32)) for j in range(2)]

        w_loaded, q_loaded, v_loaded = sem("w_loaded"), sem("q_loaded"), sem("v_loaded")
        pool_setup, dve_setup, act_setup, pe_setup = (sem(n) for n in
                                                      ("pool_setup", "dve_setup", "act_setup", "pe_setup"))
        x_loaded, y_stored = [sem("x_loaded0"), sem("x_loaded1")], [sem("y_stored0"), sem("y_stored1")]
        bn_done = {n: sem(f"bn_done_{n}") for n in LN}
        mv_done = {n: sem(f"mv_done_{n}") for n in LN}
        st_ready = {n: sem(f"st_ready_{n}") for n in LN}
        rs_done = {n: sem(f"rs_done_{n}") for n in LN}
        x0_ready, xbias_ready = sem("x0_ready"), sem("xbias_ready")
        x0_transposed, x0_hi, x0_lo = sem("x0_transposed"), sem("x0_hi"), sem("x0_lo")
        gates_ready, tanh_ready, scan_ready = sem("gates_ready"), sem("tanh_ready"), sem("scan_ready")
        ret_back, hs_ready = sem("ret_back"), sem("hs_ready")
        xhat_ready, hmul_done, hres_ready = sem("xhat_ready"), sem("hmul_done"), sem("hres_ready")
        xh_transposed, xh_hi, xh_lo = sem("xh_transposed"), sem("xh_hi"), sem("xh_lo")
        up1, gelu1, g1_hi, g1_lo = sem("up1"), sem("gelu1"), sem("g1_hi"), sem("g1_lo")
        down1, z_ready = sem("down1"), sem("z_ready")
        zn_done, zmul_done, x1_ready = sem("zn_done"), sem("zmul_done"), sem("x1_ready")
        x2_ready, x1b_ready, gback_ready = sem("x2_ready"), sem("x1b_ready"), sem("gback_ready")
        x2_transposed, x2_hi, x2_lo = sem("x2_transposed"), sem("x2_hi"), sem("x2_lo")
        up2, gelu2 = sem("up2"), sem("gelu2")
        g2_transposed, g2_hi, g2_lo = sem("g2_transposed"), sem("g2_hi"), sem("g2_lo")
        down2, centred, y_ready = sem("down2"), sem("centred"), sem("y_ready")

        block = ctx.enter_context(nc.Block())

        def steps(engine, step, first, between=None):
            for k in range(-2, first):
                if k == 1 and between:
                    between()
                step(Step(0, k))
            last = BLOCKS - 2
            with engine.Fori(0, (last - first) // 2) as pair:
                step(Step(pair, first), middle=True)
                step(Step(pair, first + 1), middle=True)
            for k in range(last, BLOCKS + 2):
                step(Step(0, k))

        def wait_alone(engine, past, past_value, semaphore, value):
            if not isinstance(value, int):
                engine.compute_val(value)
            engine.wait_ge(past, past_value)
            engine.wait_ge(semaphore, value)

        def runs(k, middle, shift):
            return middle or 0 <= k.offset + shift < BLOCKS

        def half_pairs(b):
            return b.pair + b.offset // 2

        @block.sync
        def _(sp):
            def load(k):
                sp.dma_start(x_in[:, k.parity], x_flat[bass.ts(k.value(1, 0), TOK), :]
                             .rearrange("(t p) d -> p t d", p=P)).then_inc(x_loaded[k.parity], 16)

            load(Step(0, 0))
            for dst, src in ((w1_raw, W1), (w2_raw, W2), (wret_raw, W_ret)):
                sp.dma_start(dst[:], src.rearrange("(c p) d -> p c d", p=P)).then_inc(w_loaded, 16)
            load(Step(0, 1))
            for dst, src in ((wfc_raw, W_fc), (wproj_raw, W_proj)):
                sp.dma_start(dst[:], src.rearrange("(c p) d -> p c d", p=P)).then_inc(q_loaded, 16)

            def step(k, middle=False):
                if runs(k, middle, 3) and runs(k, middle, 1):
                    sp.wait_ge(xbias_ready, k.shift(1).value(1, 1))
                    load(k.shift(3))
                if runs(k, middle, -2):
                    b = k.shift(-2)
                    sp.wait_ge(y_ready, b.value(1, 1))
                    sp.dma_start(out_flat[bass.ts(b.value(1, 0), TOK), :].rearrange("(t p) d -> p t d", p=P),
                                 y[:, b.parity]).then_inc(y_stored[b.parity], 16)

            for k in range(-1, 3):
                step(Step(0, k))
            with sp.Fori(0, (BLOCKS - 3 - 3) // 2) as pair:
                step(Step(pair, 3), middle=True)
                step(Step(pair, 4), middle=True)
            for k in range(BLOCKS - 3, BLOCKS + 2):
                step(Step(0, k))
            for s in y_stored:
                sp.wait_ge(s, 16 * BLOCKS // 2)

        @block.gpsimd
        def _(pool):
            pool.memset(ident[:], 0.0).then_inc(pool_setup, 1)
            pool.memset(ones[:], 1.0).then_inc(pool_setup, 1)
            pool.memset(halves[:], 0.5).then_inc(pool_setup, 1)
            pool.memset(expo[:], -0.5).then_inc(pool_setup, 1)
            pool.wait_ge(pool_setup, 4)
            pool.affine_select(out=ident[:], in_=ident[:], compare_op=ALU.not_equal, fill=1.0,
                               base=0, pattern=[[-1, P]], channel_multiplier=1).then_inc(pool_setup, 1)
            pool.wait_ge(dve_setup, PEAKS)
            pool.partition_all_reduce(peak_all[:], peak[:], P, bass.bass_isa.ReduceOp.max)\
                .then_inc(pool_setup, 1)
            pool.wait_ge(dve_setup, SCALES)

            def inverse_root(n, b):
                pool.wait_ge(st_ready[n], b.value(1, 1))
                pool.tensor_tensor(rstd[n][:], var_eps[n][:], expo[:], ALU.pow).then_inc(rs_done[n], 1)
                wait_alone(pool, pool_setup, 6, rs_done[n], b.value(1, 1))

            def normalise(dst, src, n, done):
                for t in range(TILES):
                    last = pool.tensor_scalar(dst[:, t], src[:, t], neg_mean[n][:, t:t + 1],
                                              rstd[n][:, t:t + 1], ALU.add, ALU.mult)
                last.then_inc(done, 1)

            def over_tiles(row):
                return row[:, None, :].to_broadcast([P, TILES, H])

            def step(k, middle=False):
                if runs(k, middle, -1):
                    b = k.shift(-1)
                    inverse_root("1", b)
                    normalise(x2, x1[:, b.parity], "1", x2_ready)
                if runs(k, middle, 1):
                    inverse_root("h", k.shift(1))
                    normalise(xhat, hs, "h", xhat_ready)
                if runs(k, middle, -1):
                    b = k.shift(-1)
                    pool.wait_ge(x2_ready, b.value(1, 1))
                    if not middle and b.offset == 0:
                        pool.wait_ge(dve_setup, SETUP_END)
                    pool.tensor_tensor(x1[:, b.parity], x1[:, b.parity], over_tiles(bp_row), ALU.add)\
                        .then_inc(x1b_ready, 1)
                if runs(k, middle, 2):
                    b = k.shift(2)
                    inverse_root("x", b)
                    normalise(x0, x_in[:, b.parity], "x", x0_ready)
                if runs(k, middle, 1):
                    b = k.shift(1)
                    pool.wait_ge(xhat_ready, b.value(1, 1))
                    pool.tensor_tensor(h_res[:, b.parity], xhat[:], over_tiles(s1_row), ALU.mult)\
                        .then_inc(hmul_done, 1)
                    pool.wait_ge(hmul_done, b.value(1, 1))
                    pool.tensor_tensor(h_res[:, b.parity], h_res[:, b.parity], over_tiles(hbias_row), ALU.add)\
                        .then_inc(hres_ready, 1)
                    pool.tensor_tensor(x_bias[:, b.parity], x_in[:, b.parity], over_tiles(bias2_row), ALU.add)\
                        .then_inc(xbias_ready, 1)
                if runs(k, middle, -1):
                    b = k.shift(-1)
                    inverse_root("g", b)
                    pool.tensor_scalar(g_back[:, b.parity], rstd["g"][:], gate_back[:, 0:1], None, ALU.mult)\
                        .then_inc(gback_ready, 1)
                if runs(k, middle, 0):
                    inverse_root("z", k)
                    normalise(zn, z, "z", zn_done)
                    pool.wait_ge(zn_done, k.value(1, 1))
                    pool.tensor_tensor(zn[:], zn[:], over_tiles(s2_row), ALU.mult).then_inc(zmul_done, 1)
                    pool.wait_ge(zmul_done, k.value(1, 1))
                    pool.tensor_tensor(x1[:, k.parity], zn[:], x_bias[:, k.parity], ALU.add)\
                        .then_inc(x1_ready, 1)

            steps(pool, step, 2)

        @block.scalar
        def _(act):
            cols = ((s1_col, ln1_scale), (bias1_col, ln1_bias), (b1_col, b1), (lnw_col, ln_w), (lnb_col, ln_b),
                    (bret_col, b_ret))
            rows = ((s1_row, ln1_scale), (hbias_row, ln1_bias), (b2_row, b2), (s2_row, ln2_scale),
                    (bias2_row, ln2_bias))
            for dst, src in cols:
                with nc.allow_non_contiguous_dma("a few hundred elements, once"):
                    act.dma_start(dst[:], src.rearrange("(c p) -> p c", p=P)).then_inc(v_loaded, 16)
            for dst, src in rows:
                act.dma_start(dst[:], src.partition_broadcast(P)).then_inc(v_loaded, 16)
            act.wait_ge(w_loaded, 16 * 3)
            act.wait_ge(dve_setup, SCALES)
            act.activation(wret_hi[:], wret_raw[:], ACT.Copy, scale=part_inv[:, 0:1]).then_inc(act_setup, 1)
            for kc in range(KC):
                act.activation(w1_hi[:, kc], w1_raw[:, kc], ACT.Copy, scale=w1_inv[:, kc:kc + 1])\
                    .then_inc(act_setup, 1)
            act.activation(w2_hi[:], w2_raw, ACT.Copy, scale=part_inv[:, 2:3]).then_inc(act_setup, 1)
            act.wait_ge(q_loaded, 16 * 2)
            for n, raw in enumerate((wfc_raw, wproj_raw)):
                act.activation(scratch[n], raw[:].rearrange("p c d -> p (c d)"), ACT.Abs,
                               accum_out=abs_sum[:, n:n + 1]).then_inc(act_setup, 1)

            def high_parts(b, dst, transposed, done):
                for m in range(KC):
                    act.wait_ge(transposed, b.value(KC, m + 1))
                    act.activation(dst[:, m], front[m][:], ACT.Copy).then_inc(done, 1)

            def gelu_and_high(k, c):
                g = ring[c % NG]
                act.wait_ge(up1, k.value(FC, c + 1))
                act.activation(g[:], g[:], ACT.Gelu_apprx_tanh, bias=b1_col[:, c:c + 1],
                               scale=w1_scale[:, 0:1]).then_inc(gelu1, 1)
                act.wait_ge(gelu1, k.value(FC, c + 1))
                act.activation(g1T_hi[:, c], g[:], ACT.Copy, scale=part_inv[:, 4:5]).then_inc(g1_hi, 1)

            def step(k, middle=False):
                for c in range(FC):
                    if runs(k, middle, 0):
                        gelu_and_high(k, c)
                    if c == X0T_AT and runs(k, middle, 1):
                        high_parts(k.shift(1), x0T_hi, x0_transposed, x0_hi)
                    if c == GATES_AT and runs(k, middle, 1):
                        for m in range(KC):
                            act.wait_ge(gates_ready, k.shift(1).value(KC, m + 1))
                            act.activation(tanh[:, m], front[m][:], ACT.Tanh, bias=bret_col[:, m:m + 1],
                                           scale=ret_scale[:, 0:1]).then_inc(tanh_ready, 1)
                    if c == X2T_AT and runs(k, middle, -1):
                        high_parts(k.shift(-1), x2T_hi, x2_transposed, x2_hi)
                for u in range(2 * TILES):
                    if runs(k, middle, -1):
                        t, half = divmod(u, 2)
                        act.wait_ge(up2, k.shift(-1).value(2 * TILES, u + 1))
                        act.activation(g2[:, t, half * HALF:(half + 1) * HALF], ring[u % NG][:], ACT.Gelu,
                                       scale=1.0 / NORM_SCALE).then_inc(gelu2, 1)
                for c in range(FC):
                    if runs(k, middle, -1):
                        act.wait_ge(g2_transposed, k.shift(-1).value(FC, c + 1))
                        act.activation(g2T_hi[:, c], ring[c % NG][:], ACT.Copy, scale=gate_col[:, c:c + 1])\
                            .then_inc(g2_hi, 1)
                    if c == XHAT_AT and runs(k, middle, 1):
                        high_parts(k.shift(1), xhT_hi, xh_transposed, xh_hi)

            steps(act, step, 2)

        @block.vector
        def _(dve):
            count = [0]

            def link(instruction):
                count[0] += 1
                instruction.then_inc(dve_setup, 1)
                dve.wait_ge(dve_setup, count[0])

            def largest(n, src):
                link(dve.tensor_reduce(out=peak[:, n:n + 1], in_=src, axis=AX_X, op=ALU.max,
                                       apply_absolute_value=True))

            dve.wait_ge(v_loaded, 16 * 11)
            dve.wait_ge(w_loaded, 16 * 3)
            link(dve.tensor_reduce(out=w1_peak[:], in_=w1_raw[:], axis=AX_X, op=ALU.max,
                                   apply_absolute_value=True))
            link(dve.tensor_tensor(w1_peak[:], w1_peak[:], s1_col[:], ALU.mult))
            dve.wait_ge(pe_setup, PE_BIAS)
            link(dve.tensor_tensor(b1_col[:], front[0][:, 0:FC], b1_col[:], ALU.add))
            for n, src in enumerate((wret_raw[:].rearrange("p c n -> p (c n)"), w1_peak[:],
                                     w2_raw.rearrange("p c n -> p (c n)"), lnw_col[:], b1_col[:])):
                largest(n, src)
            assert count[0] == PEAKS
            dve.wait_ge(pool_setup, 6)
            link(dve.scalar_tensor_tensor(peak_all[:, 4:5], peak_all[:, 1:2], float(H), peak_all[:, 4:5],
                                          ALU.mult, ALU.add))
            link(dve.tensor_scalar(peak_all[:], peak_all[:], 2.0 ** -60, None, ALU.max))
            link(dve.tensor_single_scalar(pow2[:].bitcast(U32), peak_all[:].bitcast(U32), 0x7F800000,
                                          ALU.bitwise_and))
            link(dve.reciprocal(ipow2[:], pow2[:]))
            link(dve.tensor_scalar(part_inv[:], ipow2[:], PART_SCALE, None, ALU.mult))
            link(dve.tensor_scalar(w1_inv[:], s1_col[:], part_inv[:, 1:2], None, ALU.mult))
            link(dve.tensor_scalar(ret_scale[:], pow2[:, 0:1], 0.5 / (NORM_SCALE * PART_SCALE), None, ALU.mult))
            link(dve.tensor_scalar(w1_scale[:], pow2[:, 1:2], 1.0 / (NORM_SCALE * PART_SCALE), None, ALU.mult))
            link(dve.tensor_scalar(w2_scale[:], pow2[:, 2:3], pow2[:, 4:5], None, ALU.mult))
            link(dve.tensor_scalar(w2_scale[:], w2_scale[:], PART_SCALE ** -2, None, ALU.mult))
            link(dve.tensor_scalar(gate_back[:], pow2[:, 3:4], 1.0 / GATE_SCALE, None, ALU.mult))
            link(dve.tensor_scalar(gate_col[:], lnw_col[:], ipow2[:, 3:4], GATE_SCALE, ALU.mult, ALU.mult))
            link(dve.tensor_scalar(bret_col[:], bret_col[:], 0.5, None, ALU.mult))
            link(dve.tensor_scalar(s1_row[:], s1_row[:], 1.0 / NORM_SCALE, None, ALU.mult))
            link(dve.tensor_tensor(hbias_row[:], hbias_row[:], b2_row[:], ALU.add))
            assert count[0] == SCALES
            dve.wait_ge(act_setup, 1)
            link(dve.scalar_tensor_tensor(wret_lo[:], wret_raw[:], part_inv[:, 0:1], wret_hi[:],
                                          ALU.mult, ALU.subtract))
            for kc in range(KC):
                dve.wait_ge(act_setup, 2 + kc)
                link(dve.scalar_tensor_tensor(w1_lo[:, kc], w1_raw[:, kc], w1_inv[:, kc:kc + 1], w1_hi[:, kc],
                                              ALU.mult, ALU.subtract))
            dve.wait_ge(act_setup, 2 + KC)
            link(dve.scalar_tensor_tensor(w2_lo[:], w2_raw, part_inv[:, 2:3], w2_hi[:], ALU.mult, ALU.subtract))
            assert count[0] == PARTS

            def ternary():
                dve.wait_ge(pe_setup, PE_SUMS)
                link(dve.tensor_scalar(thr[:], ring[0][:, 0:2], 0.5 / (H * F), 0.5e-6, ALU.mult, ALU.add))
                link(dve.tensor_scalar(nthr[:], thr[:], -1.0, None, ALU.mult))
                for n, raw in enumerate((wfc_raw, wproj_raw)):
                    flat = raw[:].rearrange("p c d -> p (c d)")
                    link(dve.tensor_scalar(scratch[n], flat, nthr[:, n:n + 1], None, ALU.is_lt))
                    link(dve.scalar_tensor_tensor(flat, flat, thr[:, n:n + 1], scratch[n],
                                                  ALU.is_gt, ALU.subtract))
                assert count[0] == TERNARY
                for c in range(FC):
                    link(dve.tensor_scalar(lhs_bc[0][:, c], ones[:], gate_col[:, c:c + 1], None, ALU.mult))
                    link(dve.tensor_scalar(lhs_bc[1][:, c], ones[:], lnb_col[:, c:c + 1], None, ALU.mult))
                assert count[0] == TERNARY + 2 * FC

            def ternary_back():
                for n in range(4):
                    dve.wait_ge(pe_setup, PE_SUMS + n + 1)
                    kc, c0 = n // 2, 4 * (n % 2)
                    link(dve.tensor_copy(qfc[:, kc, c0 * P:(c0 + 4) * P], ring[n][:]))
                for n in range(4):
                    dve.wait_ge(pe_setup, PE_SUMS + 4 + n + 1)
                    link(dve.tensor_copy(qproj[:, 2 * n:2 * n + 2].rearrange("p c d -> p (c d)"), ring[n][:]))
                    link(dve.tensor_copy(qproj_f[:, 2 * n:2 * n + 2].rearrange("p c d -> p (c d)"), ring[n][:]))
                assert count[0] == BACK
                dve.wait_ge(pe_setup, PE_ROWS)
                link(dve.tensor_copy(cs_row[:], acc[0][:, 0]))
                link(dve.tensor_copy(bp_row[:], acc[1][:, 0]))
                assert count[0] == SETUP_END

            def statistics(n, b, src, var_scale, eps):
                for t in range(TILES):
                    last = dve.bn_stats(bn[n][:, t], src[:, t])
                last.then_inc(bn_done[n], 1)
                aggregate(n, b, var_scale, eps, neg_mean[n][:])

            def aggregate(n, b, var_scale, eps, neg):
                wait_alone(dve, dve_setup, PARTS, bn_done[n], b.value(1, 1))
                for t in range(TILES):
                    last = dve.bn_aggr(mv[n][:, t], bn[n][:, t])
                last.then_inc(mv_done[n], 1)
                dve.wait_ge(mv_done[n], b.value(1, 1))
                dve.tensor_scalar(neg, mv[n][:, :, 0], -1.0, None, ALU.mult)
                dve.tensor_scalar(var_eps[n][:], mv[n][:, :, 1], var_scale, eps, ALU.mult, ALU.add)\
                    .then_inc(st_ready[n], 1)

            def low_parts(b, dst_hi, dst_lo, hi_done, lo_done):
                for m in range(KC):
                    dve.wait_ge(hi_done, b.value(KC, m + 1))
                    dve.tensor_tensor(dst_lo[:, m], front[m][:], dst_hi[:, m], ALU.subtract).then_inc(lo_done, 1)

            def finish(b):
                dve.wait_ge(down2, b.value(1, 1))
                for t in range(TILES):
                    last = dve.scalar_tensor_tensor(D[:, t], cs_row[:], neg_mean_g[:, b.parity, t:t + 1],
                                                    acc[t // 2][:, t % 2], ALU.mult, ALU.add)
                last.then_inc(centred, 1)

            def finish_out(b, middle):
                if middle or b.offset >= 2:
                    dve.wait_ge(y_stored[b.parity], half_pairs(b) * 16)
                dve.wait_ge(gback_ready, b.value(1, 1))
                dve.wait_ge(x1b_ready, b.value(1, 1))
                dve.wait_ge(centred, b.value(1, 1))
                for t in range(TILES):
                    last = dve.scalar_tensor_tensor(y[:, b.parity, t], D[:, t], g_back[:, b.parity, t:t + 1],
                                                    x1[:, b.parity, t], ALU.mult, ALU.add)
                last.then_inc(y_ready, 1)

            def step(k, middle=False):
                if runs(k, middle, -2):
                    finish(k.shift(-2))
                for c in range(FC):
                    if runs(k, middle, 0):
                        dve.wait_ge(g1_hi, k.value(FC, c + 1))
                        dve.scalar_tensor_tensor(g1T_lo[:, c], ring[c % NG][:], part_inv[:, 4:5], g1T_hi[:, c],
                                                 ALU.mult, ALU.subtract).then_inc(g1_lo, 1)
                    if c == 0 and runs(k, middle, -2):
                        finish_out(k.shift(-2), middle)
                    if c == X0T_AT and runs(k, middle, 1):
                        low_parts(k.shift(1), x0T_hi, x0T_lo, x0_hi, x0_lo)
                    if c == GATES_AT and runs(k, middle, 1):
                        b = k.shift(1)
                        for m in range(KC):
                            dve.wait_ge(tanh_ready, b.value(KC, m + 1))
                            first = b.parity == 0
                            dve.tensor_tensor_scan(ret[:, b.parity, m], halves[:], tanh[:, m],
                                                   -2.0 if first else ret[:, 0, m, TOK - 1:TOK],
                                                   ALU.mult, ALU.add).then_inc(scan_ready, 1)
                    if c == STAT1_AT and runs(k, middle, -1):
                        b = k.shift(-1)
                        dve.wait_ge(x1_ready, b.value(1, 1))
                        statistics("1", b, x1[:, b.parity], NORM_SCALE ** -2, EPS * NORM_SCALE ** -2)
                    if c == RET_AT and runs(k, middle, 1):
                        b = k.shift(1)
                        for j in range(2):
                            dve.wait_ge(ret_back, b.value(2, j + 1))
                            dve.scalar_tensor_tensor(hs[:, 2 * j:2 * j + 2].rearrange("p t d -> p (t d)"),
                                                     front[j][:], NORM_SCALE / 4,
                                                     x0[:, 2 * j:2 * j + 2].rearrange("p t d -> p (t d)"),
                                                     ALU.mult, ALU.add).then_inc(hs_ready, 1)
                        dve.wait_ge(hs_ready, b.value(2, 2))
                        statistics("h", b, hs, NORM_SCALE ** -2, EPS)
                    if c == X2T_AT and runs(k, middle, -1):
                        low_parts(k.shift(-1), x2T_hi, x2T_lo, x2_hi, x2_lo)
                if runs(k, middle, 2):
                    b = k.shift(2)
                    dve.wait_ge(x_loaded[b.parity], half_pairs(b) * 16 + 16)
                    statistics("x", b, x_in[:, b.parity], NORM_SCALE ** -2, EPS * NORM_SCALE ** -2)
                if runs(k, middle, 0):
                    dve.wait_ge(down1, k.value(1, 1))
                    dve.wait_ge(hres_ready, k.value(1, 1))
                    for j in range(2):
                        dve.scalar_tensor_tensor(z[:, 2 * j:2 * j + 2], acc[j][:], w2_scale[:, 0:1],
                                                 h_res[:, k.parity, 2 * j:2 * j + 2], ALU.mult, ALU.add)\
                            .then_inc(z_ready, 1)
                if runs(k, middle, -1):
                    for u in range(2 * TILES):
                        t, half = divmod(u, 2)
                        dve.wait_ge(gelu2, k.shift(-1).value(2 * TILES, u + 1))
                        last = dve.bn_stats(bn["g"][:, t, 6 * half:6 * half + 6],
                                            g2[:, t, half * HALF:(half + 1) * HALF])
                    last.then_inc(bn_done["g"], 1)
                for c in range(FC):
                    if runs(k, middle, -1):
                        dve.wait_ge(g2_hi, k.shift(-1).value(FC, c + 1))
                        dve.scalar_tensor_tensor(g2T_lo[:, c], ring[c % NG][:], gate_col[:, c:c + 1],
                                                 g2T_hi[:, c], ALU.mult, ALU.subtract).then_inc(g2_lo, 1)
                    if c == XHAT_AT and runs(k, middle, 1):
                        low_parts(k.shift(1), xhT_hi, xhT_lo, xh_hi, xh_lo)
                    if c == STATG_AT and runs(k, middle, -1):
                        b = k.shift(-1)
                        aggregate("g", b, 1.0, EPS, neg_mean_g[:, b.parity])
                    if c == STATZ_AT and runs(k, middle, 0):
                        dve.wait_ge(z_ready, k.value(2, 2))
                        statistics("z", k, z, 1.0, EPS)
                if not middle and k.offset == -1:
                    ternary()

            steps(dve, step, 4, ternary_back)

        @block.tensor
        def _(pe):
            def transposes(src, done):
                for m in range(KC):
                    for t in range(TILES):
                        last = pe.transpose(front[m][:, t * P:(t + 1) * P], src[:, t, m * P:(m + 1) * P], ident[:])
                    last.then_inc(done, 1)

            pe.wait_ge(w_loaded, 16 * 3)
            pe.wait_ge(v_loaded, 16 * 11)
            pe.wait_ge(pool_setup, 5)
            for c in range(FC):
                for kc in range(KC):
                    last = pe.matmul(front[0][:, c:c + 1], w1_raw[:, kc, c * P:(c + 1) * P], bias1_col[:, kc:kc + 1],
                                     start=(kc == 0), stop=(kc == KC - 1))
            last.then_inc(pe_setup, 1)
            pe.wait_ge(act_setup, 2 + KC + 2)
            pe.matmul(ring[0][:, 0:2], ones[:], abs_sum[:], start=True, stop=True).then_inc(pe_setup, 1)
            pe.wait_ge(dve_setup, PARTS)

            def ternary():
                pe.wait_ge(dve_setup, TERNARY)
                for kc in range(KC):
                    for c0 in (0, 4):
                        for c in range(c0, c0 + 4):
                            last = pe.transpose(ring[2 * kc + c0 // 4][:, (c - c0) * P:(c - c0 + 1) * P],
                                                wfc_raw[:, c, kc * P:(kc + 1) * P], ident[:])
                        last.then_inc(pe_setup, 1)
                for n in range(4):
                    pe.wait_ge(dve_setup, TERNARY + 2 * FC + n + 1)
                    for c in (2 * n, 2 * n + 1):
                        for kc in range(KC):
                            last = pe.transpose(ring[n][:, ((c % 2) * KC + kc) * P:((c % 2) * KC + kc + 1) * P],
                                                wproj_raw[:, kc, c * P:(c + 1) * P], ident[:])
                    last.then_inc(pe_setup, 1)
                pe.wait_ge(dve_setup, BACK)
                pe.wait_ge(z_ready, 2)
                for n in range(2):
                    for c in range(FC):
                        last = pe.matmul(acc[n][:, 0], lhs_bc[n][:, c], qproj_f[:, c],
                                         start=(c == 0), stop=(c == FC - 1))
                last.then_inc(pe_setup, 1)
                pe.wait_ge(dve_setup, SETUP_END)

            def products(dst, parts, first=True, last=True, **kw):
                for n, (lhsT, rhs) in enumerate(parts):
                    mm = pe.matmul(dst, lhsT, rhs, start=first and n == 0, stop=last and n == len(parts) - 1, **kw)
                return mm

            def up_first(k, c):
                cols = slice(c * P, (c + 1) * P)
                products(ring[c % NG][:], [
                    p for kc in range(KC) for p in ((w1_hi[:, kc, cols], xhT_hi[:, kc]),
                                                    (w1_hi[:, kc, cols], xhT_lo[:, kc]),
                                                    (w1_lo[:, kc, cols], xhT_hi[:, kc]))]).then_inc(up1, 1)

            def down_first(k, c):
                pe.wait_ge(g1_lo, k.value(FC, c + 1))
                for t in range(TILES):
                    cols = slice(t * P, (t + 1) * P)
                    mm = products(acc[t // 2][:, t % 2], ((g1T_hi[:, c, cols], w2_hi[:, c]),
                                                          (g1T_hi[:, c, cols], w2_lo[:, c]),
                                                          (g1T_lo[:, c, cols], w2_hi[:, c])),
                                  first=c == 0 and t % 2 == 0, last=c == FC - 1, skip_group_check=True)
                if c == FC - 1:
                    mm.then_inc(down1, 1)

            def up_second(b, u):
                t, half = divmod(u, 2)
                if u >= NG:
                    pe.wait_ge(gelu2, b.value(2 * TILES, u - NG + 1))
                cols = slice(t * P, (t + 1) * P)
                products(ring[u % NG][:], [
                    (part[:, kc, cols], qfc[:, kc, half * HALF:(half + 1) * HALF])
                    for kc in range(KC) for part in (x2T_hi, x2T_lo)]).then_inc(up2, 1)

            def transpose_second(b, c):
                for t in range(TILES):
                    last = pe.transpose(ring[c % NG][:, t * P:(t + 1) * P], g2[:, t, c * P:(c + 1) * P], ident[:])
                last.then_inc(g2_transposed, 1)

            def down_second(b, c):
                pe.wait_ge(g2_lo, b.value(FC, c + 1))
                for t in range(TILES):
                    cols = slice(t * P, (t + 1) * P)
                    mm = products(acc[t // 2][:, t % 2], ((g2T_hi[:, c, cols], qproj[:, c]),
                                                          (g2T_lo[:, c, cols], qproj[:, c])),
                                  first=c == 0 and t % 2 == 0, last=c == FC - 1, skip_group_check=True)
                if c == FC - 1:
                    mm.then_inc(down2, 1)

            def step(k, middle=False):
                if runs(k, middle, 0):
                    pe.wait_ge(xh_lo, k.value(KC, KC))
                if not middle and k.offset == 0:
                    pe.wait_ge(dve_setup, PARTS + 1)
                for c in range(FC + LAG):
                    if c < FC and runs(k, middle, 0):
                        up_first(k, c)
                    if c >= LAG and runs(k, middle, 0):
                        if c == LAG and (middle or k.offset >= 2):
                            pe.wait_ge(centred, k.shift(-2).value(1, 1))
                        down_first(k, c - LAG)
                    if c == X0T_AT and runs(k, middle, 1):
                        pe.wait_ge(x0_ready, k.shift(1).value(1, 1))
                        transposes(x0, x0_transposed)
                    if c == GATES_AT and runs(k, middle, 1):
                        pe.wait_ge(x0_lo, k.shift(1).value(KC, KC))
                        for m in range(KC):
                            cols = slice(m * P, (m + 1) * P)
                            products(front[m][:], [
                                p for kc in range(KC) for p in ((wret_hi[:, kc, cols], x0T_hi[:, kc]),
                                                                (wret_hi[:, kc, cols], x0T_lo[:, kc]),
                                                                (wret_lo[:, kc, cols], x0T_hi[:, kc]))])\
                                .then_inc(gates_ready, 1)
                    if c == RET_AT and runs(k, middle, 1):
                        b = k.shift(1)
                        pe.wait_ge(scan_ready, b.value(KC, KC))
                        for t in range(TILES):
                            for m in range(KC):
                                mm = pe.transpose(front[t // 2][:, (t % 2) * H + m * P:(t % 2) * H + (m + 1) * P],
                                                  ret[:, b.parity, m, t * P:(t + 1) * P], ident[:])
                            if t % 2:
                                mm.then_inc(ret_back, 1)
                    if c == X2T_AT and runs(k, middle, -1):
                        if runs(k, middle, 1):
                            pe.wait_ge(hs_ready, k.shift(1).value(2, 2))
                        pe.wait_ge(x2_ready, k.shift(-1).value(1, 1))
                        transposes(x2, x2_transposed)
                if runs(k, middle, -1):
                    pe.wait_ge(x2_lo, k.shift(-1).value(KC, KC))
                    for u in range(2 * TILES):
                        up_second(k.shift(-1), u)
                if runs(k, middle, 1):
                    pe.wait_ge(xhat_ready, k.shift(1).value(1, 1))
                    transposes(xhat, xh_transposed)
                if runs(k, middle, -1):
                    pe.wait_ge(gelu2, k.shift(-1).value(2 * TILES, 2 * TILES))
                    for c in range(FC + LAG2):
                        if c < FC:
                            transpose_second(k.shift(-1), c)
                        if c >= LAG2:
                            if c == LAG2 and runs(k, middle, 0):
                                pe.wait_ge(z_ready, k.value(2, 2))
                            down_second(k.shift(-1), c - LAG2)

            steps(pe, step, 2, ternary)


X0T_AT, GATES_AT, STAT1_AT, RET_AT, X2T_AT = 1, 3, 2, 5, 6
XHAT_AT, STATG_AT, STATZ_AT = 2, 4, 7
PEAKS = 3 + 5
SCALES = PEAKS + 15
PARTS = SCALES + 2 + KC
TERNARY = PARTS + 6
BACK = TERNARY + 2 * FC + 4 + 8
SETUP_END = BACK + 2
PE_BIAS = 1
PE_SUMS = 2
PE_ROWS = PE_SUMS + 8 + 1


_INS = ["L0_attn_x", "L0_attn_W_ret", "L0_attn_b_ret", "L0_attn_ln1_scale", "L0_attn_ln1_bias", "L0_attn_W1",
        "L0_attn_b1", "L0_attn_W2", "L0_attn_b2", "L0_attn_ln2_scale", "L0_attn_ln2_bias", "L0_ffn_W_fc",
        "L0_ffn_ln_w", "L0_ffn_ln_b", "L0_ffn_W_proj"]
_OUTS = [((16, 1024, 256), "float32")]


def kernel(**inputs):
    import numpy as _np
    import concourse.bacc as _bacc
    from concourse import mybir as _mybir
    from concourse.bass_utils import run_bass_kernel_spmd as _run

    nc = _bacc.Bacc("TRN2", target_bir_lowering=False, num_devices=1)
    arrays, args = {}, []
    for name in _INS:
        a = _np.ascontiguousarray(inputs[name])
        arrays[f"in_{name}_dram"] = a
        args.append(nc.dram_tensor(f"in_{name}_dram", a.shape, _mybir.dt.from_np(a.dtype), kind="ExternalInput").ap())
    for i, (shape, dtype) in enumerate(_OUTS):
        dt = _mybir.dt.from_np(_np.dtype(dtype))
        args.append(nc.dram_tensor(f"out_{i}_dram", shape, dt, kind="ExternalOutput").ap())
    preln_retention_ffn_ternary_kernel(nc, *args)
    r = _run(nc, [arrays], core_ids=[0])
    got = tuple(r.results[0][f"out_{i}_dram"] for i in range(len(_OUTS)))
    return got[0]
```

```python
from contextlib import ExitStack

import concourse.bass as bass
from concourse import mybir

F32 = mybir.dt.float32
F16 = mybir.dt.float16
U32 = mybir.dt.uint32
ALU = mybir.AluOpType
ACT = mybir.ActivationFunctionType
AX_X = mybir.AxisListType.X

P = 128
H = 256
F = 1024
KC = H // P
FC = F // P
TILES = 4
TOK = TILES * P
HALF = 512
NG = 4
LAG = 3
LAG2 = 3
EARLY = 2
EARLY1 = 1
SQ = 3
NORM_SCALE = 2.0 ** 10
PART_SCALE = 2.0 ** 14
GATE_SCALE = 2.0 ** 6
EPS = 1e-5


class Step:

    def __init__(self, pair, offset):
        self.pair, self.offset = pair, offset

    def shift(self, n):
        return Step(self.pair, self.offset + n)

    @property
    def parity(self):
        return self.offset % 2

    def value(self, per, n):
        return self.pair * (2 * per) + (self.offset * per + n)


def preln_retention_ffn_ternary_kernel(nc, x, W_ret, b_ret, ln1_scale, ln1_bias, W1, b1, W2, b2,
                                       ln2_scale, ln2_bias, W_fc, ln_w, ln_b, W_proj, out):
    B, S, _ = x.shape
    BLOCKS = B * S // TOK
    assert S == 2 * TOK and BLOCKS % 2 == 0
    x_flat = x.rearrange("b s d -> (b s) d")
    out_flat = out.rearrange("b s d -> (b s) d")

    with ExitStack() as ctx:
        def sb(name, shape, dt=F32):
            return ctx.enter_context(nc.sbuf_tensor(name, shape, dt))

        def sem(name):
            return ctx.enter_context(nc.semaphore(name))

        wret_hi, wret_lo = sb("wret_hi", [P, KC, H], F16), sb("wret_lo", [P, KC, H], F16)
        w1_hi, w1_lo = sb("w1_hi", [P, KC, F], F16), sb("w1_lo", [P, KC, F], F16)
        w2_hi, w2_lo = sb("w2_hi", [P, FC, H], F16), sb("w2_lo", [P, FC, H], F16)
        qfc = sb("qfc", [P, KC, F], F16)
        qproj = sb("qproj", [P, FC, H], F16)
        wret_raw, w1_raw = sb("wret_raw", [P, KC, H]), sb("w1_raw", [P, KC, F])
        wfc_raw, wproj_raw = sb("wfc_raw", [P, FC, H]), sb("wproj_raw", [P, KC, F])
        bret_col, s1_col, bias1_col = sb("bret_col", [P, KC]), sb("s1_col", [P, KC]), sb("bias1_col", [P, KC])
        b1_col, lnw_col, lnb_col = sb("b1_col", [P, FC]), sb("lnw_col", [P, FC]), sb("lnb_col", [P, FC])
        s1_row, hbias_row, b2_row = sb("s1_row", [P, H]), sb("hbias_row", [P, H]), sb("b2_row", [P, H])
        s2_row, bias2_row = sb("s2_row", [P, H]), sb("bias2_row", [P, H])
        cs_row, bp_row = sb("cs_row", [P, H]), sb("bp_row", [P, H])
        gate_col = sb("gate_col", [P, FC])
        ident, ones = sb("ident", [P, P]), sb("ones", [P, P])
        halves = sb("halves", [P, TOK])
        expo = sb("expo", [P, TILES])
        abs_sum = sb("abs_sum", [P, 2])
        thr, nthr = sb("thr", [P, 2]), sb("nthr", [P, 2])
        peak, peak_all = sb("peak", [P, 5]), sb("peak_all", [P, 5])
        pow2, ipow2 = sb("pow2", [P, 5]), sb("ipow2", [P, 5])
        part_inv = sb("part_inv", [P, 5])
        w1_peak, w1_inv = sb("w1_peak", [P, KC]), sb("w1_inv", [P, KC])
        ret_scale, w1_scale, w2_scale, gate_back = (sb(n, [P, 1]) for n in
                                                    ("ret_scale", "w1_scale", "w2_scale", "gate_back"))
        x_in, x_bias = sb("x_in", [P, 2, TILES, H]), sb("x_bias", [P, 2, TILES, H])
        x0, hs, xhat = sb("x0", [P, TILES, H]), sb("hs", [P, TILES, H]), sb("xhat", [P, TILES, H])
        h_res = sb("h_res", [P, 2, TILES, H])
        z = sb("z", [P, TILES, H])
        x1, x2 = sb("x1", [P, 2, TILES, H]), sb("x2", [P, TILES, H])
        g2 = sb("g2", [P, FC, TOK])
        square = sb("square", [P, SQ, TOK])
        g_sum = sb("g_sum", [P, 2, TOK])
        y = sb("y", [P, 2, TILES, H])
        x0T_hi, x0T_lo = sb("x0T_hi", [P, KC, TOK], F16), sb("x0T_lo", [P, KC, TOK], F16)
        xhT_hi, xhT_lo = sb("xhT_hi", [P, KC, TOK], F16), sb("xhT_lo", [P, KC, TOK], F16)
        x2T_hi, x2T_lo = sb("x2T_hi", [P, KC, TOK], F16), sb("x2T_lo", [P, KC, TOK], F16)
        tanh, ret = sb("tanh", [P, KC, TOK]), sb("ret", [P, 2, KC, TOK])
        g1T_hi, g1T_lo = sb("g1T_hi", [P, FC, TOK], F16), sb("g1T_lo", [P, FC, TOK], F16)
        g2T_hi, g2T_lo = sb("g2T_hi", [P, FC, TOK], F16), sb("g2T_lo", [P, FC, TOK], F16)
        scratch = [g2[:, 4 * n:4 * n + 4].rearrange("p c n -> p (c n)") for n in range(2)]
        qproj_f = y[:].rearrange("p s t n -> p (s t) n")
        w2_raw = x1[:].rearrange("p s t n -> p (s t) n")
        lhs_bc = g2T_hi[:].bitcast(F32).rearrange("p c (e n) -> p (c e) n", n=P)[:, 0:FC]
        LN = ("x", "h", "z", "1")
        bn = {n: sb(f"bn_{n}", [P, TILES, 6]) for n in LN}
        mv = {n: sb(f"mv_{n}", [P, TILES, 2]) for n in LN}
        neg_mean = {n: sb(f"neg_mean_{n}", [P, TILES]) for n in LN}
        var_eps = {n: sb(f"var_eps_{n}", [P, TILES]) for n in LN + ("g",)}
        rstd = {n: sb(f"rstd_{n}", [P, TILES]) for n in LN + ("g",)}
        g_back = sb("g_back", [P, TILES])
        g_total = sb("g_total", [P, 2, TILES])
        neg_mean_g, mean_sq, mean2 = (sb(n, [P, TILES]) for n in ("neg_mean_g", "mean_sq", "mean2"))

        acc = [ctx.enter_context(nc.psum_tensor(f"acc{j}", [P, 2, H], F32)) for j in range(2)]
        ring = [ctx.enter_context(nc.psum_tensor(f"ring{j}", [P, HALF], F32)) for j in range(NG)]
        front = [ctx.enter_context(nc.psum_tensor(f"front{j}", [P, HALF], F32)) for j in range(2)]

        loaded = {n: sem(f"loaded_{n}") for n in ("W_ret", "W1", "W2", "W_fc_proj", "b_ret", "b1", "ln", "rows")}
        pool_setup, dve_setup, act_setup, pe_setup = (sem(n) for n in
                                                      ("pool_setup", "dve_setup", "act_setup", "pe_setup"))
        x_loaded, y_stored = [sem("x_loaded0"), sem("x_loaded1")], [sem("y_stored0"), sem("y_stored1")]
        bn_done = {n: sem(f"bn_done_{n}") for n in LN}
        mv_done = {n: sem(f"mv_done_{n}") for n in LN}
        st_ready = {n: sem(f"st_ready_{n}") for n in LN + ("g",)}
        rs_done = {n: sem(f"rs_done_{n}") for n in LN + ("g",)}
        x0_ready, xbias_ready = sem("x0_ready"), sem("xbias_ready")
        x0_transposed, x0_hi, x0_lo = sem("x0_transposed"), sem("x0_hi"), sem("x0_lo")
        gates_ready, tanh_ready, scan_ready = sem("gates_ready"), sem("tanh_ready"), sem("scan_ready")
        ret_back, hs_ready = sem("ret_back"), sem("hs_ready")
        xhat_ready, hmul_done, hres_ready = sem("xhat_ready"), sem("hmul_done"), sem("hres_ready")
        xh_transposed, xh_hi, xh_lo = sem("xh_transposed"), sem("xh_hi"), sem("xh_lo")
        up1, gelu1, g1_hi, g1_lo = sem("up1"), sem("gelu1"), sem("g1_hi"), sem("g1_lo")
        down1, z_ready = sem("down1"), sem("z_ready")
        zn_done, zmul_done, x1_ready = sem("zn_done"), sem("zmul_done"), sem("x1_ready")
        x2_ready, x1b_ready, gback_ready = sem("x2_ready"), sem("x1b_ready"), sem("gback_ready")
        x2_transposed, x2_hi, x2_lo = sem("x2_transposed"), sem("x2_hi"), sem("x2_lo")
        up2, gelu2 = sem("up2"), sem("gelu2")
        g2_hi, g2_lo, squared = sem("g2_hi"), sem("g2_lo"), sem("squared")
        g_added, sq_added = sem("g_added"), sem("sq_added")
        g_totals, g_means, g_diff = sem("g_totals"), sem("g_means"), sem("g_diff")
        down2, centred, y_ready = sem("down2"), sem("centred"), sem("y_ready")

        block = ctx.enter_context(nc.Block())

        def steps(engine, step, start, first):
            for k in range(start, first):
                step(Step(0, k))
            last = BLOCKS - 2
            with engine.Fori(0, (last - first) // 2) as pair:
                step(Step(pair, first), middle=True)
                step(Step(pair, first + 1), middle=True)
            for k in range(last, BLOCKS + 2):
                step(Step(0, k))

        def wait_alone(engine, past, past_value, semaphore, value):
            if not isinstance(value, int):
                engine.compute_val(value)
            engine.wait_ge(past, past_value)
            engine.wait_ge(semaphore, value)

        def at(k, middle, n):
            return not middle and k.offset == n

        def x2t_at(k, middle):
            return 1 if at(k, middle, BLOCKS) else X2T_AT

        def variance_at(k, middle):
            return 7 if at(k, middle, BLOCKS) else VARIANCE_AT

        def runs(k, middle, shift):
            return middle or 0 <= k.offset + shift < BLOCKS

        def add_chunk(engine, b, n, c, src, slots, done, added):
            engine.wait_ge(done, b.value(FC, c + 1))
            if c > 1:
                engine.wait_ge(added, b.value(FC - 1, c - 1))
            engine.tensor_tensor(g_sum[:, n], src[:, 0] if c == 1 else g_sum[:, n], src[:, c % slots], ALU.add)\
                .then_inc(added, 1)

        def half_pairs(b):
            return b.pair + b.offset // 2

        @block.sync
        def _(sp):
            def load(k):
                sp.dma_start(x_in[:, k.parity], x_flat[bass.ts(k.value(1, 0), TOK), :]
                             .rearrange("(t p) d -> p t d", p=P)).then_inc(x_loaded[k.parity], 16)

            load(Step(0, 0))
            for dst, src, name in ((wret_raw, W_ret, "W_ret"), (w1_raw, W1, "W1"), (w2_raw, W2, "W2")):
                sp.dma_start(dst[:], src.rearrange("(c p) d -> p c d", p=P)).then_inc(loaded[name], 16)
            load(Step(0, 1))
            for dst, src in ((wfc_raw, W_fc), (wproj_raw, W_proj)):
                sp.dma_start(dst[:], src.rearrange("(c p) d -> p c d", p=P)).then_inc(loaded["W_fc_proj"], 16)

            def step(k, middle=False):
                if runs(k, middle, 3) and runs(k, middle, 1):
                    sp.wait_ge(xbias_ready, k.shift(1).value(1, 1))
                    load(k.shift(3))
                if runs(k, middle, -2):
                    b = k.shift(-2)
                    sp.wait_ge(y_ready, b.value(1, 1))
                    sp.dma_start(out_flat[bass.ts(b.value(1, 0), TOK), :].rearrange("(t p) d -> p t d", p=P),
                                 y[:, b.parity]).then_inc(y_stored[b.parity], 16)

            for k in range(-1, 3):
                step(Step(0, k))
            with sp.Fori(0, (BLOCKS - 3 - 3) // 2) as pair:
                step(Step(pair, 3), middle=True)
                step(Step(pair, 4), middle=True)
            for k in range(BLOCKS - 3, BLOCKS + 2):
                step(Step(0, k))
            for s in y_stored:
                sp.wait_ge(s, 16 * BLOCKS // 2)

        LAST = BLOCKS - 1

        @block.gpsimd
        def _(pool):
            pool.memset(ident[:], 0.0).then_inc(pool_setup, 1)
            pool.memset(ones[:], 1.0).then_inc(pool_setup, 1)
            pool.memset(halves[:], 0.5).then_inc(pool_setup, 1)
            pool.memset(expo[:], -0.5).then_inc(pool_setup, 1)
            pool.wait_ge(pool_setup, 4)
            pool.affine_select(out=ident[:], in_=ident[:], compare_op=ALU.not_equal, fill=1.0,
                               base=0, pattern=[[-1, P]], channel_multiplier=1).then_inc(pool_setup, 1)

            def over_partitions(n0, n1, count):
                pool.wait_ge(dve_setup, count)
                pool.partition_all_reduce(peak_all[:, n0:n1], peak[:, n0:n1], P, bass.bass_isa.ReduceOp.max)\
                    .then_inc(pool_setup, 1)

            def inverse_root(n, b):
                pool.wait_ge(st_ready[n], b.value(1, 1))
                pool.tensor_tensor(rstd[n][:], var_eps[n][:], expo[:], ALU.pow).then_inc(rs_done[n], 1)
                wait_alone(pool, pool_setup, 5, rs_done[n], b.value(1, 1))

            def normalise(dst, src, n, done):
                for t in range(TILES):
                    last = pool.tensor_scalar(dst[:, t], src[:, t], neg_mean[n][:, t:t + 1],
                                              rstd[n][:, t:t + 1], ALU.add, ALU.mult)
                last.then_inc(done, 1)

            def over_tiles(row):
                return row[:, None, :].to_broadcast([P, TILES, H])

            def step(k, middle=False):
                if runs(k, middle, -1):
                    b = k.shift(-1)
                    if not at(b, middle, LAST):
                        inverse_root("1", b)
                        normalise(x2, x1[:, b.parity], "1", x2_ready)
                    pool.wait_ge(x2_ready, b.value(1, 1))
                    if not middle and b.offset == 0:
                        pool.wait_ge(dve_setup, SETUP_END)
                    pool.tensor_tensor(x1[:, b.parity], x1[:, b.parity], over_tiles(bp_row), ALU.add)\
                        .then_inc(x1b_ready, 1)
                if runs(k, middle, 1):
                    b = k.shift(1)
                    if at(k, middle, -1):
                        pool.wait_ge(x_loaded[0], 16)
                        pool.wait_ge(loaded["rows"], 16 * 5)
                    pool.tensor_tensor(x_bias[:, b.parity], x_in[:, b.parity], over_tiles(bias2_row), ALU.add)\
                        .then_inc(xbias_ready, 1)
                if runs(k, middle, -2):
                    b = k.shift(-2)
                    inverse_root("g", b)
                    pool.tensor_scalar(g_back[:], rstd["g"][:], gate_back[:, 0:1], None, ALU.mult)\
                        .then_inc(gback_ready, 1)
                if runs(k, middle, 1):
                    b = k.shift(1)
                    inverse_root("h", b)
                    normalise(xhat, hs, "h", xhat_ready)
                if runs(k, middle, 2):
                    b = k.shift(2)
                    inverse_root("x", b)
                    normalise(x0, x_in[:, b.parity], "x", x0_ready)
                if at(k, middle, -1):
                    over_partitions(4, 5, B1_PEAK)
                    pool.wait_ge(dve_setup, ROWS)
                if runs(k, middle, 1):
                    b = k.shift(1)
                    pool.wait_ge(xhat_ready, b.value(1, 1))
                    pool.tensor_tensor(h_res[:, b.parity], xhat[:], over_tiles(s1_row), ALU.mult)\
                        .then_inc(hmul_done, 1)
                    pool.wait_ge(hmul_done, b.value(1, 1))
                    pool.tensor_tensor(h_res[:, b.parity], h_res[:, b.parity], over_tiles(hbias_row), ALU.add)\
                        .then_inc(hres_ready, 1)
                if at(k, middle, LAST):
                    inverse_root("z", k)
                    normalise(x1[:, k.parity], z, "z", zn_done)
                if runs(k, middle, -1):
                    for c in range(1, FC):
                        add_chunk(pool, k.shift(-1), 1, c, square, SQ, squared, sq_added)
                        if at(k, middle, LAST) and c == LAST_AT[1] + 1:
                            inverse_root("1", k)
                if runs(k, middle, 0) and not at(k, middle, LAST):
                    inverse_root("z", k)
                    normalise(x1[:, k.parity], z, "z", zn_done)
                    pool.wait_ge(zn_done, k.value(1, 1))
                    pool.tensor_tensor(x1[:, k.parity], x1[:, k.parity], over_tiles(s2_row), ALU.mult)\
                        .then_inc(zmul_done, 1)
                    pool.wait_ge(zmul_done, k.value(1, 1))
                    pool.tensor_tensor(x1[:, k.parity], x1[:, k.parity], x_bias[:, k.parity], ALU.add)\
                        .then_inc(x1_ready, 1)

            over_partitions(0, 1, 1)
            step(Step(0, -2))
            over_partitions(1, 4, W_PEAKS)
            steps(pool, step, -1, 2)

        @block.scalar
        def _(act):
            cols = ((bret_col, b_ret, "b_ret"), (s1_col, ln1_scale, "b1"), (bias1_col, ln1_bias, "b1"),
                    (b1_col, b1, "b1"), (lnw_col, ln_w, "ln"), (lnb_col, ln_b, "ln"))
            rows = ((s1_row, ln1_scale), (hbias_row, ln1_bias), (b2_row, b2), (s2_row, ln2_scale),
                    (bias2_row, ln2_bias))
            for dst, src, name in cols:
                with nc.allow_non_contiguous_dma("a few hundred elements, once"):
                    act.dma_start(dst[:], src.rearrange("(c p) -> p c", p=P)).then_inc(loaded[name], 16)
            for dst, src in rows:
                act.dma_start(dst[:], src.partition_broadcast(P)).then_inc(loaded["rows"], 16)
            act.wait_ge(loaded["W_ret"], 16)
            act.wait_ge(dve_setup, RET_SCALES)
            act.activation(wret_hi[:], wret_raw[:], ACT.Copy, scale=part_inv[:, 0:1]).then_inc(act_setup, 1)

            def weights_high():
                act.wait_ge(dve_setup, W_SCALES)
                act.wait_ge(loaded["W1"], 16)
                for kc in range(KC):
                    act.activation(w1_hi[:, kc], w1_raw[:, kc], ACT.Copy, scale=w1_inv[:, kc:kc + 1])\
                        .then_inc(act_setup, 1)
                act.wait_ge(loaded["W2"], 16)
                act.activation(w2_hi[:], w2_raw, ACT.Copy, scale=part_inv[:, 2:3]).then_inc(act_setup, 1)
                act.wait_ge(loaded["W_fc_proj"], 16 * 2)
                for n, raw in enumerate((wfc_raw, wproj_raw)):
                    act.activation(scratch[n], raw[:].rearrange("p c d -> p (c d)"), ACT.Abs,
                                   accum_out=abs_sum[:, n:n + 1]).then_inc(act_setup, 1)

            def ternary_back(first, last):
                for n in range(first, last):
                    act.wait_ge(pe_setup, PE_SUMS + n + 1)
                    dst = (qfc[:, n // 2, (n % 2) * HALF:(n % 2 + 1) * HALF] if n < 4 else
                           qproj[:, 2 * (n - 4):2 * (n - 4) + 2].rearrange("p c d -> p (c d)"))
                    act.activation(dst, front[n % 2][:], ACT.Copy).then_inc(act_setup, 1)

            def high_parts(b, dst, transposed, done):
                for m in range(KC):
                    act.wait_ge(transposed, b.value(KC, m + 1))
                    act.activation(dst[:, m], front[m][:], ACT.Copy).then_inc(done, 1)

            def gelu_second(b, c):
                act.wait_ge(up2, b.value(FC, c + 1))
                act.activation(g2[:, c], ring[c % NG][:], ACT.Gelu, scale=1.0 / NORM_SCALE).then_inc(gelu2, 1)

            def gelu_and_high(k, c, first):
                g = ring[c % NG]
                act.wait_ge(up1, k.value(FC, c + 1))
                act.activation(g[:], g[:], ACT.Gelu_apprx_tanh, bias=b1_col[:, c:c + 1],
                               scale=w1_scale[:, 0:1]).then_inc(gelu1, 1)
                if first:
                    act.wait_ge(dve_setup, ALL_SCALES)
                act.wait_ge(gelu1, k.value(FC, c + 1))
                act.activation(g1T_hi[:, c], g[:], ACT.Copy, scale=part_inv[:, 4:5]).then_inc(g1_hi, 1)

            def step(k, middle=False):
                if at(k, middle, 0):
                    act.wait_ge(dve_setup, B1_PEAK)
                for c in range(FC):
                    if runs(k, middle, 0):
                        gelu_and_high(k, c, at(k, middle, 0) and c == 0)
                    if at(k, middle, 0) and c == 6:
                        ternary_back(0, 2)
                    if at(k, middle, 0) and c == 7:
                        ternary_back(2, 8)
                    if c == X0T_AT and runs(k, middle, 1):
                        high_parts(k.shift(1), x0T_hi, x0_transposed, x0_hi)
                    if c == GATES_AT and runs(k, middle, 1):
                        for m in range(KC):
                            act.wait_ge(gates_ready, k.shift(1).value(KC, m + 1))
                            act.activation(tanh[:, m], front[m][:], ACT.Tanh, bias=bret_col[:, m:m + 1],
                                           scale=ret_scale[:, 0:1]).then_inc(tanh_ready, 1)
                        if at(k, middle, -1):
                            weights_high()
                    if c == x2t_at(k, middle) and runs(k, middle, -1):
                        high_parts(k.shift(-1), x2T_hi, x2_transposed, x2_hi)
                if runs(k, middle, -1):
                    gelu_second(k.shift(-1), 0)
                for c in range(FC):
                    if runs(k, middle, -1):
                        b = k.shift(-1)
                        if c + 1 < FC:
                            gelu_second(b, c + 1)
                        act.wait_ge(gelu2, b.value(FC, c + 1))
                        act.activation(g2T_hi[:, c], g2[:, c], ACT.Copy, scale=gate_col[:, c:c + 1])\
                            .then_inc(g2_hi, 1)
                        if c >= SQ:
                            act.wait_ge(sq_added, b.value(FC - 1, max(c - SQ, 1)))
                        act.activation(square[:, c % SQ], g2[:, c], ACT.Square).then_inc(squared, 1)
                    if c == XHAT_AT and runs(k, middle, 1):
                        high_parts(k.shift(1), xhT_hi, xh_transposed, xh_hi)
                if at(k, middle, 0):
                    act.wait_ge(act_setup, ACT_BANKS)
                    act.activation(qproj_f, qproj[:], ACT.Copy).then_inc(act_setup, 1)

            steps(act, step, -1, 2)

        @block.vector
        def _(dve):
            count = [0]

            def link(instruction):
                count[0] += 1
                instruction.then_inc(dve_setup, 1)
                dve.wait_ge(dve_setup, count[0])

            def largest(n, src):
                link(dve.tensor_reduce(out=peak[:, n:n + 1], in_=src, axis=AX_X, op=ALU.max,
                                       apply_absolute_value=True))

            def powers(n0, n1):
                link(dve.tensor_scalar(peak_all[:, n0:n1], peak_all[:, n0:n1], 2.0 ** -60, None, ALU.max))
                link(dve.tensor_single_scalar(pow2[:, n0:n1].bitcast(U32), peak_all[:, n0:n1].bitcast(U32),
                                              0x7F800000, ALU.bitwise_and))
                link(dve.reciprocal(ipow2[:, n0:n1], pow2[:, n0:n1]))
                link(dve.tensor_scalar(part_inv[:, n0:n1], ipow2[:, n0:n1], PART_SCALE, None, ALU.mult))

            def retention_weights():
                dve.wait_ge(pool_setup, 6)
                powers(0, 1)
                link(dve.tensor_scalar(ret_scale[:], pow2[:, 0:1], 0.5 / (NORM_SCALE * PART_SCALE), None, ALU.mult))
                dve.wait_ge(loaded["b_ret"], 16)
                link(dve.tensor_scalar(bret_col[:], bret_col[:], 0.5, None, ALU.mult))
                assert count[0] == RET_SCALES
                dve.wait_ge(act_setup, 1)
                link(dve.scalar_tensor_tensor(wret_lo[:], wret_raw[:], part_inv[:, 0:1], wret_hi[:],
                                              ALU.mult, ALU.subtract))
                assert count[0] == RET_PARTS

            def ffn_scales():
                dve.wait_ge(loaded["W1"], 16)
                dve.wait_ge(loaded["b1"], 16 * 3)
                link(dve.tensor_reduce(out=w1_peak[:], in_=w1_raw[:], axis=AX_X, op=ALU.max,
                                       apply_absolute_value=True))
                link(dve.tensor_tensor(w1_peak[:], w1_peak[:], s1_col[:], ALU.mult))
                largest(1, w1_peak[:])
                dve.wait_ge(loaded["W2"], 16)
                largest(2, w2_raw.rearrange("p c n -> p (c n)"))
                dve.wait_ge(loaded["ln"], 16 * 2)
                largest(3, lnw_col[:])
                assert count[0] == W_PEAKS
                dve.wait_ge(pool_setup, 7)
                powers(1, 4)
                link(dve.tensor_scalar(w1_inv[:], s1_col[:], part_inv[:, 1:2], None, ALU.mult))
                link(dve.tensor_scalar(w1_scale[:], pow2[:, 1:2], 1.0 / (NORM_SCALE * PART_SCALE), None, ALU.mult))
                link(dve.tensor_scalar(gate_back[:], pow2[:, 3:4], 1.0 / GATE_SCALE, None, ALU.mult))
                link(dve.tensor_scalar(gate_col[:], lnw_col[:], ipow2[:, 3:4], GATE_SCALE, ALU.mult, ALU.mult))
                assert count[0] == W_SCALES

            def w1_low():
                for kc in range(KC):
                    dve.wait_ge(act_setup, 2 + kc)
                    link(dve.scalar_tensor_tensor(w1_lo[:, kc], w1_raw[:, kc], w1_inv[:, kc:kc + 1], w1_hi[:, kc],
                                                  ALU.mult, ALU.subtract))
                assert count[0] == W1_PARTS

            def bias_scales():
                dve.wait_ge(loaded["rows"], 16 * 5)
                link(dve.tensor_scalar(s1_row[:], s1_row[:], 1.0 / NORM_SCALE, None, ALU.mult))
                link(dve.tensor_tensor(hbias_row[:], hbias_row[:], b2_row[:], ALU.add))
                assert count[0] == ROWS
                dve.wait_ge(pe_setup, PE_BIAS)
                link(dve.tensor_tensor(b1_col[:], ring[1][:, 0:FC], b1_col[:], ALU.add))
                largest(4, b1_col[:])
                assert count[0] == B1_PEAK
                dve.wait_ge(pool_setup, 8)
                link(dve.scalar_tensor_tensor(peak_all[:, 4:5], peak_all[:, 1:2], float(H), peak_all[:, 4:5],
                                              ALU.mult, ALU.add))
                powers(4, 5)
                link(dve.tensor_scalar(w2_scale[:], pow2[:, 2:3], pow2[:, 4:5], None, ALU.mult))
                link(dve.tensor_scalar(w2_scale[:], w2_scale[:], PART_SCALE ** -2, None, ALU.mult))
                assert count[0] == ALL_SCALES
                dve.wait_ge(act_setup, 2 + KC)
                link(dve.scalar_tensor_tensor(w2_lo[:], w2_raw, part_inv[:, 2:3], w2_hi[:], ALU.mult, ALU.subtract))
                assert count[0] == W2_PARTS

            def thresholds():
                dve.wait_ge(pe_setup, PE_SUMS)
                link(dve.tensor_scalar(thr[:], ring[3][:, 0:2], 0.5 / (H * F), 0.5e-6, ALU.mult, ALU.add))
                link(dve.tensor_scalar(nthr[:], thr[:], -1.0, None, ALU.mult))
                assert count[0] == THRESHOLDS

            def below(n):
                flat = (wfc_raw, wproj_raw)[n][:].rearrange("p c d -> p (c d)")
                link(dve.tensor_scalar(scratch[n], flat, nthr[:, n:n + 1], None, ALU.is_lt))

            def above(n):
                flat = (wfc_raw, wproj_raw)[n][:].rearrange("p c d -> p (c d)")
                link(dve.scalar_tensor_tensor(flat, flat, thr[:, n:n + 1], scratch[n], ALU.is_gt, ALU.subtract))
                assert count[0] == (TERNARY_FC, TERNARY_PROJ)[n]

            def broadcast(n):
                for c in range(FC):
                    link(dve.tensor_scalar(lhs_bc[:, c, n * P // 2:(n + 1) * P // 2], ones[:, 0:P // 2],
                                           (gate_col, lnb_col)[n][:, c:c + 1], None, ALU.mult))

            def rows_read():
                dve.wait_ge(pe_setup, PE_ROWS)
                link(dve.tensor_copy(qproj_f[:, 0], acc[0][:, 0]))
                assert count[0] == ROWS_READ

            def rows_spread():
                for n, row in enumerate((cs_row, bp_row)):
                    for half in range(2):
                        link(dve.tensor_copy(row[half * P // 2:(half + 1) * P // 2, :],
                                             qproj_f[n * P // 2:(n + 1) * P // 2, 0]))
                assert count[0] == SETUP_END

            setup_parts = {(-1, X0T_AT): [ffn_scales], (-1, RET_AT): [w1_low],
                           (0, 0): [thresholds, lambda: below(0)], (0, 1): [lambda: above(0)],
                           (0, 2): [lambda: below(1)], (0, 6): [lambda: above(1)],
                           (0, 7): [lambda: broadcast(0), lambda: broadcast(1)],
                           (1, 1): [rows_read], (1, 2): [rows_spread]}

            def statistics(n, b, src, var_scale, eps):
                for t in range(TILES):
                    last = dve.bn_stats(bn[n][:, t], src[:, t])
                last.then_inc(bn_done[n], 1)
                wait_alone(dve, dve_setup, 1, bn_done[n], b.value(1, 1))
                for t in range(TILES):
                    last = dve.bn_aggr(mv[n][:, t], bn[n][:, t])
                last.then_inc(mv_done[n], 1)
                dve.wait_ge(mv_done[n], b.value(1, 1))
                dve.tensor_scalar(neg_mean[n][:], mv[n][:, :, 0], -1.0, None, ALU.mult)
                dve.tensor_scalar(var_eps[n][:], mv[n][:, :, 1], var_scale, eps, ALU.mult, ALU.add)\
                    .then_inc(st_ready[n], 1)

            def statistics_x(b):
                dve.wait_ge(x_loaded[b.parity], half_pairs(b) * 16 + 16)
                statistics("x", b, x_in[:, b.parity], NORM_SCALE ** -2, EPS * NORM_SCALE ** -2)

            def low_parts(b, dst_hi, dst_lo, hi_done, lo_done):
                for m in range(KC):
                    dve.wait_ge(hi_done, b.value(KC, m + 1))
                    dve.tensor_tensor(dst_lo[:, m], front[m][:], dst_hi[:, m], ALU.subtract).then_inc(lo_done, 1)

            def row_sums(b, n):
                dve.wait_ge(g_totals, b.value(2, n + 1))
                dve.tensor_reduce(out=g_total[:, n], in_=front[n][:].rearrange("p (t n) -> p t n", n=P),
                                  axis=AX_X, op=ALU.add).then_inc(g_means, 1)

            def finish(b, middle):
                row_sums(b, 0)
                dve.wait_ge(g_means, b.value(5, 1))
                dve.tensor_scalar(neg_mean_g[:], g_total[:, 0], -1.0 / F, None, ALU.mult).then_inc(g_means, 1)
                dve.wait_ge(g_means, b.value(5, 2))
                if middle or b.offset >= 2:
                    dve.wait_ge(y_stored[b.parity], half_pairs(b) * 16)
                dve.wait_ge(down2, b.value(1, 1))
                for t in range(TILES):
                    last = dve.scalar_tensor_tensor(y[:, b.parity, t], cs_row[:], neg_mean_g[:, t:t + 1],
                                                    acc[t // 2][:, t % 2], ALU.mult, ALU.add)
                last.then_inc(centred, 1)

            def variance_g(b):
                row_sums(b, 1)
                dve.tensor_tensor(mean2[:], neg_mean_g[:], neg_mean_g[:], ALU.mult).then_inc(g_means, 1)
                dve.wait_ge(g_means, b.value(5, 4))
                dve.tensor_scalar(mean_sq[:], g_total[:, 1], 1.0 / F, EPS, ALU.mult, ALU.add).then_inc(g_means, 1)
                dve.wait_ge(g_means, b.value(5, 5))
                dve.tensor_tensor(mean2[:], mean_sq[:], mean2[:], ALU.subtract).then_inc(g_diff, 1)
                dve.wait_ge(g_diff, b.value(1, 1))
                dve.tensor_scalar(var_eps["g"][:], mean2[:], EPS, None, ALU.max).then_inc(st_ready["g"], 1)

            def finish_out(b):
                dve.wait_ge(gback_ready, b.value(1, 1))
                dve.wait_ge(x1b_ready, b.value(1, 1))
                dve.wait_ge(centred, b.value(1, 1))
                for t in range(TILES):
                    last = dve.scalar_tensor_tensor(y[:, b.parity, t], y[:, b.parity, t], g_back[:, t:t + 1],
                                                    x1[:, b.parity, t], ALU.mult, ALU.add)
                last.then_inc(y_ready, 1)

            def last_block(k, part):
                x1_k = x1[:, k.parity]
                if part == 0:
                    dve.wait_ge(zn_done, k.value(1, 1))
                    dve.tensor_tensor(x1_k, x1_k, s2_row[:, None, :].to_broadcast([P, TILES, H]), ALU.mult)\
                        .then_inc(zmul_done, 1)
                    dve.wait_ge(zmul_done, k.value(1, 1))
                    dve.wait_ge(xbias_ready, k.value(1, 1))
                    dve.tensor_tensor(x1_k, x1_k, x_bias[:, k.parity], ALU.add).then_inc(x1_ready, 1)
                elif part == 1:
                    dve.wait_ge(x1_ready, k.value(1, 1))
                    statistics("1", k, x1_k, NORM_SCALE ** -2, EPS * NORM_SCALE ** -2)
                else:
                    dve.wait_ge(rs_done["1"], k.value(1, 1))
                    for t in range(TILES):
                        last = dve.tensor_scalar(x2[:, t], x1_k[:, t], neg_mean["1"][:, t:t + 1],
                                                 rstd["1"][:, t:t + 1], ALU.add, ALU.mult)
                    last.then_inc(x2_ready, 1)

            def step(k, middle=False):
                if runs(k, middle, -2):
                    finish(k.shift(-2), middle)
                for c in range(FC):
                    if runs(k, middle, 0):
                        dve.wait_ge(g1_hi, k.value(FC, c + 1))
                        dve.scalar_tensor_tensor(g1T_lo[:, c], ring[c % NG][:], part_inv[:, 4:5], g1T_hi[:, c],
                                                 ALU.mult, ALU.subtract).then_inc(g1_lo, 1)
                    if c == variance_at(k, middle) and runs(k, middle, -2):
                        variance_g(k.shift(-2))
                    if c == FINISH_AT and runs(k, middle, -2):
                        finish_out(k.shift(-2))
                    if c == X0T_AT and runs(k, middle, 1):
                        low_parts(k.shift(1), x0T_hi, x0T_lo, x0_hi, x0_lo)
                    if c == GATES_AT and runs(k, middle, 1):
                        b = k.shift(1)
                        for m in range(KC):
                            dve.wait_ge(tanh_ready, b.value(KC, m + 1))
                            first = b.parity == 0
                            dve.tensor_tensor_scan(ret[:, b.parity, m], halves[:], tanh[:, m],
                                                   -2.0 if first else ret[:, 0, m, TOK - 1:TOK],
                                                   ALU.mult, ALU.add).then_inc(scan_ready, 1)
                    if c == (STATX_AT if not at(k, middle, -1) else RET_AT - 1) and runs(k, middle, 2):
                        statistics_x(k.shift(2))
                    if c == STAT1_AT and runs(k, middle, -1) and not at(k.shift(-1), middle, LAST):
                        b = k.shift(-1)
                        dve.wait_ge(x1_ready, b.value(1, 1))
                        statistics("1", b, x1[:, b.parity], NORM_SCALE ** -2, EPS * NORM_SCALE ** -2)
                    if c == RET_AT and runs(k, middle, 1):
                        b = k.shift(1)
                        for j in range(2):
                            dve.wait_ge(ret_back, b.value(2, j + 1))
                            dve.scalar_tensor_tensor(hs[:, 2 * j:2 * j + 2].rearrange("p t d -> p (t d)"),
                                                     front[j][:], NORM_SCALE / 4,
                                                     x0[:, 2 * j:2 * j + 2].rearrange("p t d -> p (t d)"),
                                                     ALU.mult, ALU.add).then_inc(hs_ready, 1)
                        dve.wait_ge(hs_ready, b.value(2, 2))
                        statistics("h", b, hs, NORM_SCALE ** -2, EPS)
                    if c == x2t_at(k, middle) and runs(k, middle, -1):
                        low_parts(k.shift(-1), x2T_hi, x2T_lo, x2_hi, x2_lo)
                    if not middle:
                        for part in setup_parts.get((k.offset, c), ()):
                            part()
                if runs(k, middle, 0):
                    dve.wait_ge(down1, k.value(1, 1))
                    dve.wait_ge(hres_ready, k.value(1, 1))
                    for j in range(2):
                        dve.scalar_tensor_tensor(z[:, 2 * j:2 * j + 2], acc[j][:], w2_scale[:, 0:1],
                                                 h_res[:, k.parity, 2 * j:2 * j + 2], ALU.mult, ALU.add)\
                            .then_inc(z_ready, 1)
                for c in range(FC):
                    if runs(k, middle, -1):
                        b = k.shift(-1)
                        if c > 0:
                            add_chunk(dve, b, 0, c, g2, FC, gelu2, g_added)
                        dve.wait_ge(g2_hi, b.value(FC, c + 1))
                        dve.scalar_tensor_tensor(g2T_lo[:, c], g2[:, c], gate_col[:, c:c + 1],
                                                 g2T_hi[:, c], ALU.mult, ALU.subtract).then_inc(g2_lo, 1)
                    if c == XHAT_AT and runs(k, middle, 1):
                        low_parts(k.shift(1), xhT_hi, xhT_lo, xh_hi, xh_lo)
                    if at(k, middle, LAST) and c in LAST_AT:
                        last_block(k, LAST_AT.index(c))
                    if c == (0 if at(k, middle, LAST) else STATZ_AT) and runs(k, middle, 0):
                        dve.wait_ge(z_ready, k.value(2, 2))
                        statistics("z", k, z, 1.0, EPS)
                if at(k, middle, -1):
                    bias_scales()

            dve.wait_ge(loaded["W_ret"], 16)
            largest(0, wret_raw[:].rearrange("p c n -> p (c n)"))
            statistics_x(Step(0, 0))
            retention_weights()
            steps(dve, step, -1, 4)

        @block.tensor
        def _(pe):
            def transposes(src, done):
                for m in range(KC):
                    for t in range(TILES):
                        last = pe.transpose(front[m][:, t * P:(t + 1) * P], src[:, t, m * P:(m + 1) * P], ident[:])
                    last.then_inc(done, 1)

            def bias_products(c0, c1):
                pe.wait_ge(loaded["W1"], 16)
                pe.wait_ge(loaded["b1"], 16 * 3)
                for c in range(c0, c1):
                    for kc in range(KC):
                        last = pe.matmul(ring[1][:, c:c + 1], w1_raw[:, kc, c * P:(c + 1) * P],
                                         bias1_col[:, kc:kc + 1], start=(kc == 0), stop=(kc == KC - 1))
                if c1 == FC:
                    last.then_inc(pe_setup, 1)

            def ternary_transposes(n):
                if n == 0:
                    pe.wait_ge(hs_ready, 2 * 2)
                if n in (0, 4):
                    pe.wait_ge(dve_setup, (TERNARY_FC, TERNARY_PROJ)[n // 4])
                if n >= 2:
                    pe.wait_ge(act_setup, ACT_SUMS + n - 1)
                for i in range(4):
                    if n < 4:
                        kc, c = n // 2, 4 * (n % 2) + i
                        src = wfc_raw[:, c, kc * P:(kc + 1) * P]
                    else:
                        c, kc = 2 * (n - 4) + i // KC, i % KC
                        src = wproj_raw[:, kc, c * P:(c + 1) * P]
                    last = pe.transpose(front[n % 2][:, i * P:(i + 1) * P], src, ident[:])
                last.then_inc(pe_setup, 1)

            def ternary_rows():
                pe.wait_ge(act_setup, ACT_BANKS + 1)
                pe.wait_ge(dve_setup, BROADCASTS)
                pe.wait_ge(z_ready, 2)
                for c in range(FC):
                    last = pe.matmul(acc[0][:, 0], lhs_bc[:, c], qproj_f[:, c], start=(c == 0), stop=(c == FC - 1))
                last.then_inc(pe_setup, 1)
                pe.wait_ge(dve_setup, ROWS_READ)

            def products(dst, parts, first=True, last=True, **kw):
                for n, (lhsT, rhs) in enumerate(parts):
                    mm = pe.matmul(dst, lhsT, rhs, start=first and n == 0, stop=last and n == len(parts) - 1, **kw)
                return mm

            def up_first(k, c):
                cols = slice(c * P, (c + 1) * P)
                products(ring[c % NG][:], [
                    p for kc in range(KC) for p in ((w1_hi[:, kc, cols], xhT_hi[:, kc]),
                                                    (w1_hi[:, kc, cols], xhT_lo[:, kc]),
                                                    (w1_lo[:, kc, cols], xhT_hi[:, kc]))]).then_inc(up1, 1)

            def down_first(k, c):
                pe.wait_ge(g1_lo, k.value(FC, c + 1))
                for t in range(TILES):
                    cols = slice(t * P, (t + 1) * P)
                    mm = products(acc[t // 2][:, t % 2], ((g1T_hi[:, c, cols], w2_hi[:, c]),
                                                          (g1T_hi[:, c, cols], w2_lo[:, c]),
                                                          (g1T_lo[:, c, cols], w2_hi[:, c])),
                                  first=c == 0 and t % 2 == 0, last=c == FC - 1, skip_group_check=True)
                if c == FC - 1:
                    mm.then_inc(down1, 1)

            def up_second(b, c):
                if c >= NG:
                    pe.wait_ge(gelu2, b.value(FC, c - NG + 1))
                products(ring[c % NG][:], [
                    (qfc[:, kc, c * P:(c + 1) * P], part[:, kc])
                    for kc in range(KC) for part in (x2T_hi, x2T_lo)]).then_inc(up2, 1)

            def totals(b, n):
                pe.wait_ge((g_added, sq_added)[n], b.value(FC - 1, FC - 1))
                for t in range(TILES):
                    last = pe.transpose(front[n][:, t * P:(t + 1) * P], g_sum[:, n, t * P:(t + 1) * P], ident[:])
                last.then_inc(g_totals, 1)

            def down_second(b, c):
                pe.wait_ge(g2_lo, b.value(FC, c + 1))
                for t in range(TILES):
                    cols = slice(t * P, (t + 1) * P)
                    mm = products(acc[t // 2][:, t % 2], ((g2T_hi[:, c, cols], qproj[:, c]),
                                                          (g2T_lo[:, c, cols], qproj[:, c])),
                                  first=c == 0 and t % 2 == 0, last=c == FC - 1, skip_group_check=True)
                if c == FC - 1:
                    mm.then_inc(down2, 1)

            def starts_early(k, middle):
                return middle or k.offset > 1

            def step(k, middle=False):
                if runs(k, middle, 0) and not starts_early(k, middle):
                    pe.wait_ge(xh_lo, k.value(KC, KC))
                if at(k, middle, 0):
                    pe.wait_ge(dve_setup, W1_PARTS)
                for c in range(FC + LAG):
                    if at(k, middle, 0) and c in (1, 3):
                        pe.wait_ge(dve_setup, B1_PEAK if c == 1 else THRESHOLDS)
                    if c < FC and runs(k, middle, 0) and not (c < EARLY1 and starts_early(k, middle)):
                        up_first(k, c)
                    if c >= LAG and runs(k, middle, 0):
                        if c == LAG and (middle or k.offset >= 2):
                            pe.wait_ge(centred, k.shift(-2).value(1, 1))
                        if at(k, middle, 0) and c == LAG:
                            pe.wait_ge(dve_setup, W2_PARTS)
                        if at(k, middle, 1) and c == LAG:
                            ternary_rows()
                        down_first(k, c - LAG)
                    if c == 0 and runs(k, middle, -2):
                        totals(k.shift(-2), 0)
                    if c == variance_at(k, middle) and runs(k, middle, -2):
                        if runs(k, middle, 1):
                            pe.wait_ge(tanh_ready, k.shift(1).value(KC, KC))
                        if at(k, middle, BLOCKS):
                            pe.wait_ge(x2_lo, k.shift(-1).value(KC, KC))
                        totals(k.shift(-2), 1)
                    if c == X0T_AT and runs(k, middle, 1):
                        if runs(k, middle, -2):
                            pe.wait_ge(g_means, k.shift(-2).value(5, 1))
                        pe.wait_ge(x0_ready, k.shift(1).value(1, 1))
                        transposes(x0, x0_transposed)
                    if c == GATES_AT and runs(k, middle, 1):
                        if at(k, middle, -1):
                            pe.wait_ge(dve_setup, RET_PARTS)
                        pe.wait_ge(x0_lo, k.shift(1).value(KC, KC))
                        for m in range(KC):
                            cols = slice(m * P, (m + 1) * P)
                            products(front[m][:], [
                                p for kc in range(KC) for p in ((wret_hi[:, kc, cols], x0T_hi[:, kc]),
                                                                (wret_hi[:, kc, cols], x0T_lo[:, kc]),
                                                                (wret_lo[:, kc, cols], x0T_hi[:, kc]))])\
                                .then_inc(gates_ready, 1)
                        if at(k, middle, -1):
                            bias_products(0, FC // 2)
                    if c == RET_AT and runs(k, middle, 1):
                        b = k.shift(1)
                        if runs(k, middle, -2):
                            pe.wait_ge(g_means, k.shift(-2).value(5, 4))
                        pe.wait_ge(scan_ready, b.value(KC, KC))
                        for t in range(TILES):
                            for m in range(KC):
                                mm = pe.transpose(front[t // 2][:, (t % 2) * H + m * P:(t % 2) * H + (m + 1) * P],
                                                  ret[:, b.parity, m, t * P:(t + 1) * P], ident[:])
                            if t % 2:
                                mm.then_inc(ret_back, 1)
                        if at(k, middle, -1):
                            bias_products(FC // 2, FC)
                    if c == x2t_at(k, middle) and runs(k, middle, -1):
                        if runs(k, middle, 1):
                            pe.wait_ge(hs_ready, k.shift(1).value(2, 2))
                        else:
                            pe.wait_ge(g_means, k.shift(-2).value(5, 1 if at(k, middle, BLOCKS) else 4))
                        pe.wait_ge(x2_ready, k.shift(-1).value(1, 1))
                        transposes(x2, x2_transposed)
                    if at(k, middle, 0) and FC - 2 <= c < FC + 2:
                        ternary_transposes(2 * (c - FC + 2))
                        ternary_transposes(2 * (c - FC + 2) + 1)
                    ahead = c - (FC + LAG - 1 - EARLY)
                    if 0 <= ahead < EARLY and runs(k, middle, -1):
                        if ahead == 0:
                            pe.wait_ge(x2_lo, k.shift(-1).value(KC, KC))
                        up_second(k.shift(-1), ahead)
                for c in range(EARLY, FC + LAG2):
                    if runs(k, middle, -1):
                        if c < FC:
                            up_second(k.shift(-1), c)
                        if c >= LAG2:
                            if c == LAG2 and runs(k, middle, 0):
                                pe.wait_ge(z_ready, k.value(2, 2))
                            ahead = c - (FC + LAG2 - 1 - EARLY1)
                            if 0 <= ahead < EARLY1 and runs(k, middle, 1) and starts_early(k.shift(1), middle):
                                if ahead == 0:
                                    pe.wait_ge(xh_lo, k.shift(1).value(KC, KC))
                                up_first(k.shift(1), ahead)
                            down_second(k.shift(-1), c - LAG2)
                    if c == XHAT_AT and runs(k, middle, 1):
                        if at(k, middle, 0):
                            pe.wait_ge(act_setup, ACT_BANKS)
                        pe.wait_ge(xhat_ready, k.shift(1).value(1, 1))
                        transposes(xhat, xh_transposed)
                        if at(k, middle, -1):
                            pe.wait_ge(act_setup, ACT_SUMS)
                            pe.matmul(ring[3][:, 0:2], ones[:], abs_sum[:], start=True, stop=True)\
                                .then_inc(pe_setup, 1)

            pe.wait_ge(pool_setup, 5)
            steps(pe, step, -1, 2)


X0T_AT, GATES_AT, STAT1_AT, RET_AT, X2T_AT = 1, 3, 2, 5, 6
VARIANCE_AT, FINISH_AT, STATX_AT = 4, 7, 2
XHAT_AT, STATZ_AT = 2, 7
LAST_AT = (2, 3, 5)
RET_SCALES = 7
RET_PARTS = RET_SCALES + 1
W_PEAKS = RET_PARTS + 2 + 3
W_SCALES = W_PEAKS + 4 + 4
W1_PARTS = W_SCALES + KC
ROWS = W1_PARTS + 2
B1_PEAK = ROWS + 2
ALL_SCALES = B1_PEAK + 1 + 4 + 2
W2_PARTS = ALL_SCALES + 1
THRESHOLDS = W2_PARTS + 2
TERNARY_FC = THRESHOLDS + 2
TERNARY_PROJ = TERNARY_FC + 2
BROADCASTS = TERNARY_PROJ + 2 * FC
ROWS_READ = BROADCASTS + 1
SETUP_END = ROWS_READ + 4
ACT_SUMS = 1 + KC + 1 + 2
ACT_BANKS = ACT_SUMS + 8
PE_BIAS = 1
PE_SUMS = 2
PE_ROWS = PE_SUMS + 8 + 1


_INS = ["L0_attn_x", "L0_attn_W_ret", "L0_attn_b_ret", "L0_attn_ln1_scale", "L0_attn_ln1_bias", "L0_attn_W1",
        "L0_attn_b1", "L0_attn_W2", "L0_attn_b2", "L0_attn_ln2_scale", "L0_attn_ln2_bias", "L0_ffn_W_fc",
        "L0_ffn_ln_w", "L0_ffn_ln_b", "L0_ffn_W_proj"]
_OUTS = [((16, 1024, 256), "float32")]


def kernel(**inputs):
    import numpy as _np
    import concourse.bacc as _bacc
    from concourse import mybir as _mybir
    from concourse.bass_utils import run_bass_kernel_spmd as _run

    nc = _bacc.Bacc("TRN2", target_bir_lowering=False, num_devices=1)
    arrays, args = {}, []
    for name in _INS:
        a = _np.ascontiguousarray(inputs[name])
        arrays[f"in_{name}_dram"] = a
        args.append(nc.dram_tensor(f"in_{name}_dram", a.shape, _mybir.dt.from_np(a.dtype), kind="ExternalInput").ap())
    for i, (shape, dtype) in enumerate(_OUTS):
        dt = _mybir.dt.from_np(_np.dtype(dtype))
        args.append(nc.dram_tensor(f"out_{i}_dram", shape, dt, kind="ExternalOutput").ap())
    preln_retention_ffn_ternary_kernel(nc, *args)
    r = _run(nc, [arrays], core_ids=[0])
    got = tuple(r.results[0][f"out_{i}_dram"] for i in range(len(_OUTS)))
    return got[0]
```
